# Optimizing a Trainium2 kernel written in Bass

```python
import numpy as np
import jax
import jax.numpy as jnp

def _softmax(x, axis=-1):
    return jax.nn.softmax(x, axis=axis)
def _gelu(x):
    return jax.nn.gelu(x, approximate=True)
def _silu(x):
    return jax.nn.silu(x)
def _sigmoid(x):
    return jax.nn.sigmoid(x)
def _layernorm(x, axis=-1, eps=1e-5):
    m = jnp.mean(x, axis=axis, keepdims=True)
    v = jnp.var(x, axis=axis, keepdims=True)
    return (x - m) / jnp.sqrt(v + eps)
def _scatter_add(tgt, idx, src, axis=0):
    return tgt.at[idx].add(src)
def _segment_sum(src, seg, n):
    return jax.ops.segment_sum(src, seg, n)

kernel_name = 'mk_conv_seq_d1_conv_nchw512_a58089'

def setup_inputs(seed: int = 0):
    np.random.seed(seed)
    _w = jnp.asarray
    def _rec_inputs():
        import jax
        import jax.numpy as jnp
        _gk = jax.random.key(seed)
        x = 7.22e-05 + 1 * jax.random.normal(jax.random.fold_in(_gk, 1), (16, 512, 32, 32), jnp.float32)
        return x
    x = _rec_inputs()
    def _L0_conv_setup():
        import math
        import jax, jax.numpy as jnp
        import numpy as np
        B, C, H, W = (16, 512, 32, 32)
        NUM_HEADS = 8
        NUM_GROUPS = 32
        EPS = 1e-05
        key = jax.random.key(seed)
        ks = jax.random.split(key, 5)
        x = jax.random.normal(ks[0], (B, C, H, W), dtype=jnp.float32)
        norm_g = jnp.ones((C,), jnp.float32)
        norm_b = jnp.zeros((C,), jnp.float32)
        qkv_w = jax.random.normal(ks[1], (3 * C, C), dtype=jnp.float32) * (1.0 / math.sqrt(C))
        qkv_b = jnp.zeros((3 * C,), jnp.float32)
        proj_w = jax.random.normal(ks[2], (C, C), dtype=jnp.float32) * (1.0 / math.sqrt(C))
        proj_b = jnp.zeros((C,), jnp.float32)
        return {'x': x, 'norm_g': norm_g, 'norm_b': norm_b, 'qkv_w': qkv_w, 'qkv_b': qkv_b, 'proj_w': proj_w, 'proj_b': proj_b}
    _L0_conv_all = _L0_conv_setup()
    _L0_conv_in = {k: v for k, v in _L0_conv_all.items() if k in ('norm_g', 'norm_b', 'qkv_w', 'qkv_b', 'proj_w', 'proj_b', )}
    del _L0_conv_all

    return {
        "x": x,
        "L0_conv_norm_g": _L0_conv_in["norm_g"],
        "L0_conv_norm_b": _L0_conv_in["norm_b"],
        "L0_conv_qkv_w": _L0_conv_in["qkv_w"],
        "L0_conv_qkv_b": _L0_conv_in["qkv_b"],
        "L0_conv_proj_w": _L0_conv_in["proj_w"],
        "L0_conv_proj_b": _L0_conv_in["proj_b"],
    }

def reference(x, L0_conv_norm_g, L0_conv_norm_b, L0_conv_qkv_w, L0_conv_qkv_b, L0_conv_proj_w, L0_conv_proj_b):
    import jax
    import jax.numpy as jnp
    def _L0_conv_ref(x, norm_g, norm_b, qkv_w, qkv_b, proj_w, proj_b):
        import math
        import jax, jax.numpy as jnp
        import numpy as np
        B, C, H, W = (16, 512, 32, 32)
        NUM_HEADS = 8
        NUM_GROUPS = 32
        EPS = 1e-05
        b, c = (x.shape[0], x.shape[1])
        spatial = x.shape[2:]
        s = int(np.prod(spatial))
        xf = x.reshape(b, c, s)
        xg = xf.reshape(b, NUM_GROUPS, c // NUM_GROUPS, s).astype(jnp.float32)
        mean = xg.mean(axis=(2, 3), keepdims=True)
        var = xg.var(axis=(2, 3), keepdims=True)
        xn = ((xg - mean) * jax.lax.rsqrt(var + EPS)).reshape(b, c, s)
        xn = (xn * norm_g[None, :, None] + norm_b[None, :, None]).astype(x.dtype)
        qkv = jnp.einsum('oc,bcs->bos', qkv_w, xn) + qkv_b[None, :, None]
        hd = c // NUM_HEADS
        q, k, v = jnp.split(qkv, 3, axis=1)
        q = q.reshape(b, NUM_HEADS, hd, s)
        k = k.reshape(b, NUM_HEADS, hd, s)
        v = v.reshape(b, NUM_HEADS, hd, s)
        scale = 1.0 / math.sqrt(math.sqrt(hd))
        w = jnp.einsum('bhct,bhcs->bhts', q * scale, k * scale)
        w = jax.nn.softmax(w.astype(jnp.float32), axis=-1).astype(qkv.dtype)
        a = jnp.einsum('bhts,bhcs->bhct', w, v).reshape(b, c, s)
        h = jnp.einsum('oc,bcs->bos', proj_w, a) + proj_b[None, :, None]
        return (xf + h).reshape(b, c, *spatial)

    def _gn(v, G=32, eps=1e-5):
        B_, C_, H_, W_ = v.shape
        g = v.reshape(B_, G, C_ // G, H_, W_)
        m = jnp.mean(g, axis=(2, 3, 4), keepdims=True)
        s = jnp.var(g, axis=(2, 3, 4), keepdims=True)
        return ((g - m) / jnp.sqrt(s + eps)).reshape(v.shape)

    def _ln_c(v, eps=1e-6):
        m = jnp.mean(v, axis=1, keepdims=True)
        s = jnp.var(v, axis=1, keepdims=True)
        return (v - m) / jnp.sqrt(s + eps)

    def _ln_t(v, eps=1e-5):
        m = jnp.mean(v, axis=-1, keepdims=True)
        s = jnp.var(v, axis=-1, keepdims=True)
        return (v - m) / jnp.sqrt(s + eps)

    def _to_tokens(v):
        B_, C_, H_, W_ = v.shape
        return v.reshape(B_, C_, H_ * W_).transpose(0, 2, 1)
    def _from_tokens(t, like):
        B_, C_, H_, W_ = like.shape
        return t.transpose(0, 2, 1).reshape(B_, C_, H_, W_)

    x = _L0_conv_ref(x, L0_conv_norm_g, L0_conv_norm_b, L0_conv_qkv_w, L0_conv_qkv_b, L0_conv_proj_w, L0_conv_proj_b)
    return x


_drawn_inputs = setup_inputs


def setup_inputs(seed=0):
    import zlib

    import numpy as np

    out = dict(_drawn_inputs(seed))
    spreads = {'L0_conv_norm_g': (1.0, 0.2),
     'L0_conv_norm_b': (0.0, 0.1),
     'L0_conv_qkv_b': (0.0, 0.1),
     'L0_conv_proj_b': (0.0, 0.1)}
    factors = {}
    for name, (base, spread) in spreads.items():
        noise = np.random.default_rng([zlib.crc32(name.encode()), seed]).standard_normal(out[name].shape)
        drawn = base * np.exp(spread * noise) if base else spread * noise
        out[name] = jnp.asarray(drawn.astype(out[name].dtype))
    for name, factor in factors.items():
        out[name] = (out[name] * factor).astype(out[name].dtype)
    return out
```

```python
from contextlib import ExitStack

import concourse.bass as bass
from concourse import mybir

F32 = mybir.dt.float32
F16 = mybir.dt.float16
ACT = mybir.ActivationFunctionType
ALU = mybir.AluOpType
AX = mybir.AxisListType

P = 128
HEADS = 8
GROUPS = 32
EPS = 1e-5
W_SCALE = 2.0 ** 8

STATS_STEPS = [2, 6, 10, 14]
NORMALISE_STEPS = [42, 44, 47, 49]
X_STEPS = [0, 0, 3, 7, 11, 15, 44, 46]


def begun(count):
    return not isinstance(count, int) or count > 0


def dense_schedule():
    out = []
    for n, (kind, part) in enumerate([("q", 0), ("q", 1), ("k", 0), ("k", 1), ("v", 0), ("v", 1), ("p", 0), ("p", 1)]):
        out.append((2 * n, 2 * n + 1, kind, 1, part))
    steps = [(16, 16), (17, 17), (18, 19), (20, 20), (21, 21), (22, 23), (24, 24), (25, 25), (26, 26),
             (27, 27), (28, 28), (29, 29), (30, 30), (31, 31)]
    kinds = [("q", 0), ("q", 1), ("p", 2), ("k", 0), ("k", 1), ("p", 3), ("p", 4), ("v", 0), ("v", 1),
             ("g", 0), ("p", 5), ("p", 6), ("p", 7), ("g", 1)]
    out += [(a, z, kind, 2, part) for (a, z), (kind, part) in zip(steps, kinds)]
    qkv = [("q", 0), ("q", 1), ("k", 0), ("k", 1), ("v", 0), ("v", 1)]
    steps = [(32, 32), (33, 34), (35, 35), (36, 37), (40, 40), (41, 41)]
    out += [(a, z, kind, 3, part) for (a, z), (kind, part) in zip(steps, qkv)]
    steps = [(52, 52), (53, 53), (54, 55), (56, 57), (58, 59), (60, 61)]
    out += [(a, z, kind, 4, part) for (a, z), (kind, part) in zip(steps, qkv)]
    return out


def attention_block(nc, x, norm_g, norm_b, qkv_wT, qkv_b, proj_wT, proj_b, out):
    B, C, S = x.shape
    CT = C // P
    HD = C // HEADS
    ST = S // P
    HALF = S // 2
    NT = 2 * ST
    TB = NT * CT
    HB = TB // 8
    QKV_SCALE = 1.0 / W_SCALE
    ATT_SCALE = 1.0 / float(HD) ** 0.5
    assert (CT, HD, ST, NT) == (4, 64, 8, 16)

    DENSE = dense_schedule()
    PER_BATCH = len(DENSE)
    N_PROJ = 2 * CT
    BEFORE = [(0, 0, kind, 4, part) for kind in "gqkv" for part in range(2)]
    FIRST_DENSE = len(BEFORE)
    assert FIRST_DENSE == N_PROJ

    def dense_of(first, last):
        kept = [d for d in DENSE if not (first and d[2] == "p") and not (last and (d[2] == "g" or d[3] == 4))]
        return list(enumerate(kept))

    def dense_base(b):
        return FIRST_DENSE if isinstance(b, int) and b == 0 else b * PER_BATCH

    def place_of(first, last, kind, pair, part):
        return next(i for i, d in dense_of(first, last) if d[2:] == (kind, pair, part))

    with ExitStack() as ctx:
        def sb(name, shape, dt=F32):
            return ctx.enter_context(nc.sbuf_tensor(name, shape, dt))

        def psum(name, shape, dt=F32):
            return ctx.enter_context(nc.psum_tensor(name, shape, dt))

        def sem(name):
            return ctx.enter_context(nc.semaphore(name))

        w_qkv = sb("w_qkv", [P, 2, CT, 3 * C], F16)
        w_proj = sb("w_proj", [P, 2, CT, C], F16)
        x_in = sb("x_in", [P, 2, S])
        xn = sb("xn", [P, 2, CT, S], F16)
        qkv32 = sb("qkv32", [P, 2, HALF])
        q_nat = sb("q_nat", [P, 2, S], F16)
        k_nat = sb("k_nat", [P, 2, S], F16)
        q_st = sb("q_st", [P, 2, 2, S], F16)
        k_st = sb("k_st", [P, 2, 2, 2, S], F16)
        v_sb = sb("v_sb", [P, 2, ST, 2, P], F16)
        probs = sb("probs", [P, 2, S])
        pT = sb("pT", [P, 2, 2, ST, 2, HALF], F16)
        spread = sb("spread", [P, HALF // P, 2, HD])
        recip_rows = sb("recip_rows", [P, HALF])
        att32 = sb("att32", [P, HALF])
        att = sb("att", [P, 2, CT, S], F16)
        att_first = sb("att_first", [P, 2, S], F16)
        resid = sb("resid", [P, 2, HALF])
        out_sb = sb("out_sb", [P, 2, HALF])
        ident = sb("ident", [P, P])
        group_mean = sb("group_mean", [P, P])
        neg_max = sb("neg_max", [P, 4])
        row_sum = sb("row_sum", [P, 2, 8])
        recip = sb("recip", [P, 8])
        stats = sb("stats", [P, CT, 2, 6])
        mean_var = sb("mean_var", [P, CT, 2])
        g_mean = sb("g_mean", [P, CT])
        dev = sb("dev", [P, CT])
        dev2 = sb("dev2", [P, CT])
        c_var = sb("c_var", [P, CT])
        g_var = sb("g_var", [P, CT])
        rstd = sb("rstd", [P, CT])
        minus_half = sb("minus_half", [P, CT])
        xn_scale = sb("xn_scale", [P, CT])
        xn_shift = sb("xn_shift", [P, CT])
        mean_scaled = sb("mean_scaled", [P, CT])
        g_sb = sb("g_sb", [P, CT])
        b_sb = sb("b_sb", [P, CT])
        qkvb_sb = sb("qkvb_sb", [P, 3 * CT])
        qb_scaled = sb("qb_scaled", [P, CT])
        projb_sb = sb("projb_sb", [P, CT])
        w_in = pT[:].rearrange("p a b c d e -> p (a b c d e)").bitcast(F32)
        w_qkv_in = w_in[:, 0:CT * 3 * C].rearrange("p (c o) -> p c o", c=CT)
        w_proj_in = w_in[:, CT * 3 * C:CT * 4 * C].rearrange("p (c o) -> p c o", c=CT)

        scores = psum("scores", [P, 2, S])
        turned = psum("turned", [P, 2, HALF])
        att_acc = psum("att_acc", [P, HALF])
        dense = psum("dense", [P, HALF])

        small_in = sem("small_in")
        w_loaded = sem("w_loaded")
        x_loaded = [sem("x_loaded0"), sem("x_loaded1")]
        const_steps = sem("const_steps")
        const_ready = sem("const_ready")
        w_hi = sem("w_hi")
        w_ready = sem("w_ready")
        gn_done = sem("gn_done")
        rstd_ready = sem("rstd_ready")
        xn_hi = sem("xn_hi")
        xn_lo = sem("xn_lo")
        dense_done = sem("dense_done")
        qkv_hi = sem("qkv_hi")
        qkv_lo = sem("qkv_lo")
        q_stacked = sem("q_stacked")
        k_stacked = sem("k_stacked")
        scores_ready = sem("scores_ready")
        max_ready = sem("max_ready")
        probs_ready = sem("probs_ready")
        turned_ready = sem("turned_ready")
        pT_hi = sem("pT_hi")
        pT_lo = sem("pT_lo")
        recip_ready = sem("recip_ready")
        spread_ready = sem("spread_ready")
        rows_turned = sem("rows_turned")
        rows_ready = sem("rows_ready")
        att_done = sem("att_done")
        att_scaled = sem("att_scaled")
        att_biased = sem("att_biased")
        att_hi = sem("att_hi")
        att_lo = sem("att_lo")
        att_moved = sem("att_moved")
        proj_biased = sem("proj_biased")
        res_loaded = [sem("res_loaded0"), sem("res_loaded1")]
        out_ready = sem("out_ready")
        out_free = [sem("out_free0"), sem("out_free1")]

        block = ctx.enter_context(nc.Block())

        def in_loop(engine, batch):
            batch(0, True, False)
            with engine.Fori(1, B - 1) as b:
                batch(b, False, False)
            batch(B - 1, False, True)

        @block.tensor
        def _(pe):
            def split_product(dst, w, r, n, count):
                for j, (i, k) in enumerate(((0, 0), (1, 0), (0, 1))):
                    last = nc.tensor.matmul(dst, w(i), r(k), start=n == 0 and j == 0, stop=n == count - 1 and j == 2)
                return last

            def dense_part(kind, pair, part, half):
                h = pair % CT
                if kind == "g":
                    src = mean_var[:, :, 0] if part == 0 else c_var[:, :]
                    return nc.tensor.matmul(dense[:, 0:CT], group_mean[:, :], src, start=True, stop=True)
                if kind == "v":
                    for s in range(2 * half, 2 * half + 2):
                        k0 = (4 * part + s) * P
                        for c in range(CT):
                            last = split_product(dense[:, s * P:(s + 1) * P],
                                                 lambda i: xn[:, i, c, k0:k0 + P],
                                                 lambda i: w_qkv[:, i, c, 2 * C + h * P:2 * C + (h + 1) * P], c, CT)
                    return last
                for c in range(2 * half, 2 * half + 2):
                    if kind == "p":
                        o, n0 = part // 2, part % 2 * HALF
                        last = split_product(dense[:, :], lambda i: w_proj[:, i, c, o * P:(o + 1) * P],
                                             lambda i: att[:, i, c, n0:n0 + HALF], c, CT)
                    else:
                        o = (0 if kind == "q" else C) + h * P
                        last = split_product(dense[:, :], lambda i: w_qkv[:, i, c, o:o + P],
                                             lambda i: xn[:, i, c, part * HALF:(part + 1) * HALF], c, CT)
                return last

            def wait_bank_left(b, before):
                _, _, kind, pair, part = before
                if kind == "p":
                    pe.wait_ge(proj_biased, N_PROJ * b - N_PROJ + part + 1)
                elif kind == "g":
                    pe.wait_ge(gn_done, 20 * b + (33, 37)[part])
                else:
                    pe.wait_ge(qkv_hi, 48 * b + 12 * pair + 4 * "qkv".index(kind) + 2 * part + 2)

            def dense_step(b, step, chunk):
                first, final, kind, pair, part = chunk
                if step == first:
                    if kind == "q" and pair == 4 and part == 0:
                        pe.wait_ge(xn_lo, CT * b + 2 * CT)
                    if kind == "g":
                        pe.wait_ge(gn_done, 20 * b + (32 if part == 0 else 36))
                    if kind == "p" and part == 0:
                        pe.wait_ge(att_lo, HB * b)
                        pe.wait_ge(att_moved, 16 * b)
                halves = [0] if kind == "g" else [0, 1] if first == final else [0 if step == first else 1]
                for half in halves:
                    last = dense_part(kind, pair, part, half)
                if step == final:
                    last.then_inc(dense_done, 1)

            def score_tile(t):
                buf, head, q0 = t // NT % 2, t % 2, t % NT // 2 * P
                for bank in range(2):
                    for part in range(2):
                        last = nc.tensor.matmul(scores[:, t % 2, bank * HALF:(bank + 1) * HALF],
                                                q_st[:, buf, head, q0:q0 + P],
                                                k_st[:, buf, head, part, bank * HALF:(bank + 1) * HALF],
                                                start=part == 0, stop=part == 1)
                last.then_inc(scores_ready, 1)

            def attend(t, s):
                half = t // 8 - 1
                buf = half // 2 % 2
                for j, (i, k) in enumerate(((0, 0), (1, 0), (0, 1))):
                    for head in range(2):
                        last = nc.tensor.matmul(att_acc[head * HD:(head + 1) * HD, :],
                                                v_sb[:, buf, s, i, head * HD:(head + 1) * HD],
                                                pT[:, half % 2, k, s, head, :],
                                                start=s == 0 and j == 0, stop=s == ST - 1 and j == 2)
                if s == ST - 1:
                    last.then_inc(att_done, 1)

            def turn_rows():
                for q in range(HALF // P):
                    last = nc.tensor.transpose(turned[:, 0, q * P:(q + 1) * P],
                                               spread[:, q, :, :].rearrange("p h d -> p (h d)"), ident[:, :])
                last.then_inc(rows_turned, 1)

            def batch(b, first, final):
                for t in range(TB):
                    pe.wait_ge(probs_ready, TB * b + t + 1)
                    if not (final and t + 2 >= TB):
                        if (t + 2) % NT == 0:
                            pair = (t + 2) // NT
                            pe.wait_ge(q_stacked, 64 * CT * b + 64 * (pair + 1))
                            pe.wait_ge(k_stacked, 64 * CT * b + 64 * (pair + 1))
                        score_tile(t + 2)
                    for bank in range(2):
                        if begun(count := 2 * TB * b + 2 * t + bank - 1):
                            pe.wait_ge(pT_lo, count)
                        if t % 8 == 5 and bank == 0 and not (first and t < 8):
                            pe.wait_ge(rows_ready, HB * b + t // 8)
                        for s in range(4):
                            k0 = (4 * bank + s) * P
                            last = nc.tensor.transpose(turned[:, bank, s * P:(s + 1) * P],
                                                       probs[:, t % 2, k0:k0 + P], ident[:, :])
                        last.then_inc(turned_ready, 1)
                    for i, chunk in dense_of(first, final):
                        if t == chunk[0]:
                            if i == 0:
                                wait_bank_left(b - 1, BEFORE[-1])
                            else:
                                wait_bank_left(b, dense_of(first, final)[i - 1][1])
                        if chunk[0] <= t <= chunk[1]:
                            dense_step(b, t, chunk)
                    if not (first and t < 8):
                        if t % 8 == 0:
                            pe.wait_ge(pT_lo, 2 * TB * b + 2 * t)
                            if begun(count := HB * b + t // 8 - 1):
                                pe.wait_ge(att_scaled, count)
                        if t % 16 == 8:
                            pe.wait_ge(qkv_lo, 24 * b + 6 * (t // NT) + 6)
                        attend(t, t % 8)
                        if t % 8 == 4:
                            pe.wait_ge(spread_ready, HB * b + t // 8)
                            pe.wait_ge(pT_lo, 2 * TB * b + 2 * t + 1)
                            turn_rows()

            pe.wait_ge(const_ready, 1)
            for i, chunk in enumerate(BEFORE):
                if i == 2:
                    pe.wait_ge(w_ready, 2 * CT)
                if i:
                    wait_bank_left(-1, BEFORE[i - 1])
                dense_step(-1, 0, chunk)
            pe.wait_ge(q_stacked, 64)
            pe.wait_ge(k_stacked, 64)
            score_tile(0)
            score_tile(1)
            in_loop(pe, batch)
            pe.wait_ge(pT_lo, 2 * TB * B)
            pe.wait_ge(att_scaled, HB * B - 1)
            for s in range(ST):
                attend(TB, s)
            pe.wait_ge(spread_ready, HB * B)
            turn_rows()
            for part in range(N_PROJ):
                if part == 0:
                    wait_bank_left(B - 1, dense_of(False, True)[-1][1])
                else:
                    wait_bank_left(B, (0, 0, "p", 1, part - 1))
                dense_step(B, 0, (0, 0, "p", 1, part))

        @block.scalar
        def _(act):
            def drain_dense(b, number, chunk):
                _, _, kind, pair, part = chunk
                if kind == "g":
                    return
                h = pair % CT
                act.wait_ge(dense_done, number + 1)
                if kind == "p":
                    act.wait_ge(out_free[part % 2], 64 * b - 48 + 16 * (part // 2))
                    nc.scalar.activation(out_sb[:, part % 2, :], dense[:, :], ACT.Identity,
                                         bias=projb_sb[:, part // 2:part // 2 + 1], scale=QKV_SCALE)\
                        .then_inc(proj_biased, 1)
                    return
                n = "qkv".index(kind) * 2 + part
                if begun(count := 24 * b + 6 * pair + n - 1):
                    act.wait_ge(qkv_lo, count)
                if kind == "v":
                    src = dense[:, :].rearrange("p (s c) -> p s c", c=P)
                    full = qkv32[:, part, :].rearrange("p (s c) -> p s c", c=P)
                    hi = v_sb[:, pair % 2, 4 * part:4 * part + 4, 0, :]
                    if begun(count := HB * b + 2 * pair - 2):
                        act.wait_ge(att_done, count)
                    scale, bias = QKV_SCALE, 0.0
                else:
                    src, full = dense[:, :], qkv32[:, part, :]
                    nat, stacked = (q_nat, q_stacked) if kind == "q" else (k_nat, k_stacked)
                    hi = nat[:, 0, part * HALF:(part + 1) * HALF]
                    if begun(count := 64 * CT * b + 64 * pair):
                        act.wait_ge(stacked, count)
                    if kind == "q":
                        scale, bias = QKV_SCALE * ATT_SCALE, qb_scaled[:, h:h + 1]
                    else:
                        scale, bias = QKV_SCALE, qkvb_sb[:, CT + h:CT + h + 1]
                nc.scalar.activation(full, src, ACT.Identity, bias=bias, scale=scale).then_inc(qkv_hi, 1)
                nc.scalar.activation(hi, src, ACT.Identity, bias=bias, scale=scale)\
                    .then_inc(qkv_hi, 1)

            def normalise(b, c):
                buf = c % 2
                act.wait_ge(x_loaded[buf], 64 * b + 112 + 16 * (c // 2))
                act.wait_ge(gn_done, 20 * b + 40)
                nc.scalar.activation(x_in[:, buf, :], x_in[:, buf, :], ACT.Identity,
                                     bias=xn_shift[:, c:c + 1], scale=xn_scale[:, c:c + 1]).then_inc(xn_hi, 1)
                act.wait_ge(xn_hi, 8 * b + 8 + 2 * c + 1)
                nc.scalar.activation(xn[:, 0, c, :], x_in[:, buf, :], ACT.Copy).then_inc(xn_hi, 1)

            def exp_tile(b, t):
                act.wait_ge(max_ready, TB * b + t + 1)
                if t % 8 == 0:
                    if begun(count := HB * b + t // 8 - 1):
                        act.wait_ge(recip_ready, count)
                nc.scalar.activation(probs[:, t % 2, :], scores[:, t % 2, :], ACT.Exp,
                                     bias=neg_max[:, t % 4:t % 4 + 1],
                                     accum_out=row_sum[:, t // 8 % 2, t % 8:t % 8 + 1]).then_inc(probs_ready, 1)

            def turned_hi(b, t, bank):
                act.wait_ge(turned_ready, 2 * TB * b + 2 * t + bank + 1)
                if t % 8 == 0 and bank == 0:
                    if begun(count := HB * b + t // 8 - 1):
                        act.wait_ge(att_done, count)
                q0 = t % 8 // 2 * P
                nc.scalar.activation(pT[:, t // 8 % 2, 0, 4 * bank:4 * bank + 4, t % 2, q0:q0 + P],
                                     turned[:, bank, :].rearrange("p (s q) -> p s q", q=P), ACT.Copy).then_inc(pT_hi, 1)

            def spread_recip(b, half):
                act.wait_ge(recip_ready, HB * b + half + 1)
                if begun(count := HB * b + half):
                    act.wait_ge(rows_turned, count)
                nc.scalar.activation(spread[:, :, :, :].rearrange("p q h d -> p (q h) d"),
                                     recip[:, :].unsqueeze(2).to_broadcast([P, 8, HD]), ACT.Copy).then_inc(spread_ready, 1)

            def keep_rows(b, half):
                act.wait_ge(rows_turned, HB * b + half + 1)
                if begun(count := HB * b + half):
                    act.wait_ge(att_scaled, count)
                nc.scalar.activation(recip_rows[:, :], turned[:, 0, :], ACT.Copy).then_inc(rows_ready, 1)

            def att_split_hi(b, half, att_read=0):
                pair, n0 = half // 2, half % 2 * HALF
                act.wait_ge(att_scaled, HB * b + half + 1)
                nc.scalar.activation(att32[:, :], att32[:, :], ACT.Identity,
                                     bias=qkvb_sb[:, 2 * CT + pair:2 * CT + pair + 1]).then_inc(att_biased, 1)
                act.wait_ge(att_biased, HB * b + half + 1)
                if half == 0:
                    if begun(count := 16 * b):
                        act.wait_ge(att_moved, count)
                if begun(count := att_read):
                    act.wait_ge(dense_done, count)
                dst = att_first[:, 0, n0:n0 + HALF] if pair == 0 else att[:, 0, pair, n0:n0 + HALF]
                nc.scalar.activation(dst, att32[:, :], ACT.Copy).then_inc(att_hi, 1)

            def batch(b, first, final):
                for t in range(TB):
                    if t % 8 == 5 and not (first and t < 8):
                        keep_rows(b, t // 8 - 1)
                    for bank in range(2):
                        turned_hi(b, t, bank)
                    if not (final and t + 2 >= TB):
                        exp_tile(b, t + 2)
                    for i, chunk in dense_of(first, final):
                        if chunk[1] == t:
                            drain_dense(b, dense_base(b) + i, chunk)
                    if t % 8 == 1 and not (first and t < 16):
                        if t == 33 and not first:
                            att_split_hi(b, 2, dense_base(b) + place_of(first, final, "p", 2, 7) + 1)
                        elif t >= 16:
                            att_split_hi(b, t // 8 - 2)
                        else:
                            att_split_hi(b - 1, HB - 2 + t // 8)
                    if t % 8 == 2 and not (first and t < 8):
                        spread_recip(b, t // 8 - 1)
                    if not final and t in NORMALISE_STEPS:
                        c = NORMALISE_STEPS.index(t)
                        if c == 0:
                            act.wait_ge(dense_done, dense_base(b) + place_of(first, final, "v", 3, 1) + 1)
                        normalise(b, c)

            act.wait_ge(small_in, 48)
            act.wait_ge(out_free[0], 16)
            act.wait_ge(out_free[1], 16)
            nc.scalar.mul(qb_scaled[:, :], qkvb_sb[:, 0:CT], ATT_SCALE).then_inc(w_hi, 1)
            act.wait_ge(w_loaded, 16 * 2 * CT)
            for c in range(CT):
                nc.scalar.activation(w_qkv[:, 0, c, :], w_qkv_in[:, c, :], ACT.Copy, scale=W_SCALE).then_inc(w_hi, 1)
                nc.scalar.activation(w_proj[:, 0, c, :], w_proj_in[:, c, :], ACT.Copy, scale=W_SCALE).then_inc(w_hi, 1)
            for c in range(CT):
                normalise(-1, c)
            act.wait_ge(w_hi, 1)
            for i, chunk in enumerate(BEFORE):
                drain_dense(-1, i, chunk)
            exp_tile(0, 0)
            exp_tile(0, 1)
            in_loop(act, batch)
            att_split_hi(B - 1, HB - 2)
            spread_recip(B - 1, HB - 1)
            keep_rows(B - 1, HB - 1)
            att_split_hi(B - 1, HB - 1)
            base = PER_BATCH * (B - 1) + len(dense_of(False, True))
            for part in range(N_PROJ):
                drain_dense(B, base + part, (0, 0, "p", 1, part))

        @block.vector
        def _(dve):
            def gn_stats(b, c):
                dve.wait_ge(x_loaded[c % 2], 64 * b + 80 + 16 * (c // 2))
                for n in range(2):
                    nc.vector.bn_stats(stats[:, c, n, :], x_in[:, c % 2, n * HALF:(n + 1) * HALF]).then_inc(gn_done, 1)

            def gn_aggregate(c):
                nc.vector.bn_aggr(mean_var[:, c, :], stats[:, c, :, :]).then_inc(gn_done, 1)

            def gn_mean(b, number):
                n0 = 20 * b + 20
                dve.wait_ge(dense_done, number + 1)
                if begun(count := 8 * b + 8):
                    dve.wait_ge(xn_hi, count)
                nc.vector.tensor_copy(g_mean[:, :], dense[:, 0:CT]).then_inc(gn_done, 1)
                dve.wait_ge(gn_done, n0 + 13)
                nc.vector.tensor_tensor(dev[:, :], mean_var[:, :, 0], g_mean[:, :], ALU.subtract).then_inc(gn_done, 1)
                dve.wait_ge(gn_done, n0 + 14)
                nc.vector.tensor_tensor(dev2[:, :], dev[:, :], dev[:, :], ALU.mult).then_inc(gn_done, 1)
                dve.wait_ge(gn_done, n0 + 15)
                nc.vector.tensor_tensor(c_var[:, :], dev2[:, :], mean_var[:, :, 1], ALU.add).then_inc(gn_done, 1)

            def gn_affine(b, number):
                n0 = 20 * b + 20
                dve.wait_ge(dense_done, number + 1)
                nc.vector.tensor_scalar(g_var[:, :], dense[:, 0:CT], EPS, None, ALU.add)\
                    .then_inc(gn_done, 1)
                dve.wait_ge(rstd_ready, b + 2)
                nc.vector.tensor_tensor(xn_scale[:, :], rstd[:, :], g_sb[:, :], ALU.mult).then_inc(gn_done, 1)
                dve.wait_ge(gn_done, n0 + 18)
                nc.vector.tensor_tensor(mean_scaled[:, :], g_mean[:, :], xn_scale[:, :], ALU.mult).then_inc(gn_done, 1)
                dve.wait_ge(gn_done, n0 + 19)
                nc.vector.tensor_tensor(xn_shift[:, :], b_sb[:, :], mean_scaled[:, :], ALU.subtract).then_inc(gn_done, 1)

            def max_tile(b, t):
                dve.wait_ge(scores_ready, TB * b + t + 1)
                nc.vector.tensor_reduce(neg_max[:, t % 4:t % 4 + 1], scores[:, t % 2, :], AX.X, ALU.max,
                                        negate=True).then_inc(max_ready, 1)

            def turned_lo(b, t, bank):
                dve.wait_ge(pT_hi, 2 * TB * b + 2 * t + bank + 1)
                q0 = t % 8 // 2 * P
                part = [pT[:, t // 8 % 2, i, 4 * bank:4 * bank + 4, t % 2, q0:q0 + P] for i in range(2)]
                nc.vector.tensor_tensor(part[1], turned[:, bank, :].rearrange("p (s q) -> p s q", q=P), part[0],
                                        ALU.subtract).then_inc(pT_lo, 1)

            def scale_att(b, half):
                dve.wait_ge(att_done, HB * b + half + 1)
                dve.wait_ge(rows_ready, HB * b + half + 1)
                if begun(count := HB * b + half):
                    dve.wait_ge(att_lo, count)
                nc.vector.tensor_tensor(att32[:, :], att_acc[:, :], recip_rows[:, :], ALU.mult).then_inc(att_scaled, 1)

            def invert_sums(b, half):
                dve.wait_ge(probs_ready, TB * b + 8 * half + 8)
                if begun(count := HB * b + half):
                    dve.wait_ge(spread_ready, count)
                nc.vector.reciprocal(recip[:, :], row_sum[:, half % 2, :]).then_inc(recip_ready, 1)

            def batch(b, first, final):
                for t in range(TB):
                    if t % 8 == 0 and not (first and t < 16):
                        if t >= 16:
                            scale_att(b, t // 8 - 2)
                        else:
                            scale_att(b - 1, HB - 2 + t // 8)
                    aggregate = not final and t - 1 in STATS_STEPS
                    if aggregate:
                        c = STATS_STEPS.index(t - 1)
                        dve.wait_ge(gn_done, 20 * b + 20 + 3 * c + 2)
                    if not (final and t + 2 >= TB):
                        max_tile(b, t + 2)
                    if aggregate:
                        gn_aggregate(c)
                    for bank in range(2):
                        turned_lo(b, t, bank)
                    if t % 8 == 0 and not (first and t < 8):
                        if t >= 8:
                            invert_sums(b, t // 8 - 1)
                        else:
                            invert_sums(b - 1, HB - 1)
                    if not final and t in STATS_STEPS:
                        gn_stats(b, STATS_STEPS.index(t))
                    for i, chunk in dense_of(first, final):
                        if chunk[1] == t and chunk[2] == "g":
                            (gn_mean, gn_affine)[chunk[4]](b, dense_base(b) + i)

            for c in range(CT):
                gn_stats(-1, c)
                dve.wait_ge(gn_done, 3 * c + 2)
                gn_aggregate(c)
            dve.wait_ge(small_in, 48)
            gn_mean(-1, 0)
            gn_affine(-1, 1)
            for c in range(CT):
                dve.wait_ge(w_hi, 2 * c + 3)
                nc.vector.scalar_tensor_tensor(w_qkv[:, 1, c, :], w_qkv_in[:, c, :], W_SCALE, w_qkv[:, 0, c, :],
                                               ALU.mult, ALU.subtract).then_inc(w_ready, 1)
                nc.vector.scalar_tensor_tensor(w_proj[:, 1, c, :], w_proj_in[:, c, :], W_SCALE,
                                               w_proj[:, 0, c, :], ALU.mult, ALU.subtract).then_inc(w_ready, 1)
            max_tile(0, 0)
            max_tile(0, 1)
            in_loop(dve, batch)
            scale_att(B - 1, HB - 2)
            invert_sums(B - 1, HB - 1)
            scale_att(B - 1, HB - 1)

        @block.gpsimd
        def _(pool):
            def qkv_split_lo(b, chunk):
                _, _, kind, pair, part = chunk
                n = "qkv".index(kind) * 2 + part
                pool.wait_ge(qkv_hi, 48 * b + 12 * pair + 2 * n + 2)
                if kind == "v":
                    full = qkv32[:, part, :].rearrange("p (s c) -> p s c", c=P)
                    hi, lo = (v_sb[:, pair % 2, 4 * part:4 * part + 4, i, :] for i in range(2))
                else:
                    nat = q_nat if kind == "q" else k_nat
                    full = qkv32[:, part, :]
                    hi, lo = (nat[:, i, part * HALF:(part + 1) * HALF] for i in range(2))
                nc.gpsimd.tensor_tensor(lo, full, hi, ALU.subtract).then_inc(qkv_lo, 1)

            def xn_split_lo(b, c):
                pool.wait_ge(xn_hi, 8 * b + 8 + 2 * c + 2)
                nc.gpsimd.tensor_tensor(xn[:, 1, c, :], x_in[:, c % 2, :], xn[:, 0, c, :], ALU.subtract)\
                    .then_inc(xn_lo, 1)

            def att_split_lo(b, half):
                pair, n0 = half // 2, half % 2 * HALF
                pool.wait_ge(att_hi, HB * b + half + 1)
                hi, lo = ((att_first[:, i, n0:n0 + HALF] if pair == 0 else att[:, i, pair, n0:n0 + HALF]) for i in range(2))
                nc.gpsimd.tensor_tensor(lo, att32[:, :], hi, ALU.subtract).then_inc(att_lo, 1)

            def add_residual(b, part):
                pool.wait_ge(res_loaded[part % 2], 64 * b - 64 + 16 * (part // 2) + 16)
                pool.wait_ge(proj_biased, N_PROJ * b - N_PROJ + part + 1)
                nc.gpsimd.tensor_tensor(out_sb[:, part % 2, :], out_sb[:, part % 2, :], resid[:, part % 2, :], ALU.add)\
                    .then_inc(out_ready, 1)

            def invert_std(b):
                pool.wait_ge(gn_done, 20 * b + 37)
                nc.gpsimd.tensor_tensor(rstd[:, :], g_var[:, :], minus_half[:, :], ALU.pow).then_inc(rstd_ready, 1)

            def batch(b, first, final):
                for t in range(TB):
                    for i, chunk in dense_of(first, final):
                        if chunk[1] == t:
                            if chunk[2] in "qkv":
                                qkv_split_lo(b, chunk)
                            elif chunk[2] == "p":
                                add_residual(b, chunk[4])
                            elif chunk[4] == 1:
                                invert_std(b)
                    if t % 8 == 1 and not (first and t < 16):
                        if t >= 16:
                            att_split_lo(b, t // 8 - 2)
                        else:
                            att_split_lo(b - 1, HB - 2 + t // 8)
                    if not final and t in NORMALISE_STEPS:
                        xn_split_lo(b, NORMALISE_STEPS.index(t))

            nc.gpsimd.memset(ident[:, :], 0.0).then_inc(const_steps, 1)
            nc.gpsimd.memset(group_mean[:, :], GROUPS / C).then_inc(const_steps, 1)
            nc.gpsimd.memset(minus_half[:, :], -0.5).then_inc(const_steps, 1)
            pool.wait_ge(const_steps, 3)
            nc.gpsimd.affine_select(out=ident[:, :], in_=ident[:, :], compare_op=ALU.not_equal, fill=1.0, base=0,
                                    pattern=[[-1, P]], channel_multiplier=1).then_inc(const_steps, 1)
            per = C // GROUPS
            blocks = group_mean[:, :].rearrange("p (g c) -> p g c", c=per)
            nc.gpsimd.affine_select(out=blocks, in_=blocks, compare_op=ALU.is_ge, fill=0.0, base=0,
                                    pattern=[[-per, P // per], [0, per]], channel_multiplier=1).then_inc(const_steps, 1)
            pool.wait_ge(const_steps, 5)
            nc.gpsimd.affine_select(out=blocks, in_=blocks, compare_op=ALU.is_ge, fill=0.0, base=per - 1,
                                    pattern=[[per, P // per], [0, per]], channel_multiplier=-1).then_inc(const_ready, 1)
            invert_std(-1)
            for c in range(CT):
                xn_split_lo(-1, c)
            for chunk in BEFORE[2:]:
                qkv_split_lo(-1, chunk)
            in_loop(pool, batch)
            att_split_lo(B - 1, HB - 2)
            att_split_lo(B - 1, HB - 1)
            for part in range(N_PROJ):
                add_residual(B, part)

        @block.sync
        def _(sp):
            def row(ap, b):
                return ap[bass.ds(b, 1)].rearrange("o c s -> (o c) s")

            def load_x(b, k):
                c, buf = k % CT, k % 2
                if k < 2:
                    if begun(count := CT * b + 3 + k):
                        sp.wait_ge(xn_lo, count)
                elif k < 6:
                    sp.wait_ge(gn_done, 20 * b + 20 + 3 * (k - 2) + 3)
                else:
                    sp.wait_ge(xn_lo, CT * b + CT + k - 5)
                sp.dma_start(x_in[:, buf, :], row(x, b + 1)[c * P:(c + 1) * P, :]).then_inc(x_loaded[buf], 16)

            def stack_q(b, pair):
                buf, h = pair % 2, HD
                sp.wait_ge(qkv_lo, 24 * b + 6 * pair + 2)
                for dst, head, src, part in ((0, 0, 0, 0), (h, 0, 0, 1), (0, 1, h, 1), (h, 1, h, 0)):
                    sp.dma_start(q_st[dst:dst + h, buf, head, :], q_nat[src:src + h, part, :]).then_inc(q_stacked, 16)

            def stack_k(b, pair):
                buf, h = pair % 2, HD
                sp.wait_ge(qkv_lo, 24 * b + 6 * pair + 4)
                for head in range(2):
                    for dst in (0, h):
                        sp.dma_start(k_st[dst:dst + h, buf, head, :, :], k_nat[head * h:(head + 1) * h, :, :])\
                            .then_inc(k_stacked, 16)

            def load_residual(b, part):
                o, n0 = part // 2, part % 2 * HALF
                if part < 2:
                    sp.wait_ge(out_free[part], 64 * b - 48)
                else:
                    sp.wait_ge(out_ready, N_PROJ * b - N_PROJ + part - 1)
                sp.dma_start(resid[:, part % 2, :], row(x, b - 1)[o * P:(o + 1) * P, n0:n0 + HALF])\
                    .then_inc(res_loaded[part % 2], 16)

            def store(b, part):
                o, n0 = part // 2, part % 2 * HALF
                sp.wait_ge(out_ready, N_PROJ * b - N_PROJ + part + 1)
                sp.dma_start(row(out, b - 1)[o * P:(o + 1) * P, n0:n0 + HALF], out_sb[:, part % 2, :])\
                    .then_inc(out_free[part % 2], 16)

            def move_first(b, first, final):
                sp.wait_ge(att_lo, HB * b + 2)
                if not first:
                    sp.wait_ge(dense_done, dense_base(b) + place_of(first, final, "p", 2, 7) + 1)
                sp.dma_start(att[:, :, 0, :], att_first[:, :, :]).then_inc(att_moved, 16)

            def batch(b, first, final):
                for t in range(TB):
                    for i, chunk in dense_of(first, final):
                        _, ended, kind, pair, part = chunk
                        if kind == "p" and ended - 3 == t:
                            load_residual(b, part)
                        if ended + 1 == t and kind in "qk" and part == 1:
                            (stack_q if kind == "q" else stack_k)(b, pair)
                        if ended + 1 == t and kind == "p":
                            store(b, part)
                    if not final and t in X_STEPS:
                        for k in [k for k, s in enumerate(X_STEPS) if s == t]:
                            load_x(b, k)
                    if t == 33:
                        move_first(b, first, final)

            for k in range(2):
                load_x(-1, k)
            for dst, src in ((g_sb, norm_g), (b_sb, norm_b), (qkvb_sb, qkv_b)):
                sp.dma_start(dst[:, :], src).then_inc(small_in, 16)
            for n in range(2):
                cols = slice(n * CT // 2, (n + 1) * CT // 2)
                sp.dma_start(projb_sb[:, cols], proj_b[:, cols]).then_inc(out_free[n], 16)
            for c in range(CT):
                sp.dma_start(w_qkv_in[:, c, :], qkv_wT[c * P:(c + 1) * P, :]).then_inc(w_loaded, 16)
            for k in range(2, 6):
                load_x(-1, k)
            for c in range(CT):
                sp.dma_start(w_proj_in[:, c, :], proj_wT[c * P:(c + 1) * P, :]).then_inc(w_loaded, 16)
            for k in range(6, 8):
                load_x(-1, k)
            stack_q(-1, 4)
            stack_k(-1, 4)
            in_loop(sp, batch)
            for part in range(2):
                load_residual(B, part)
            for part in range(N_PROJ):
                store(B, part)
                if part + 2 < N_PROJ:
                    load_residual(B, part + 2)
            for buf in range(2):
                sp.wait_ge(out_free[buf], 16 + 64 * B)


def kernel(**inputs):
    import numpy as np
    import concourse.bacc as bacc
    from concourse.bass_utils import run_bass_kernel_spmd

    x = np.asarray(inputs["x"])
    B, C, H, W = x.shape

    def columns(v):
        return np.ascontiguousarray(np.asarray(v).reshape(-1, P).T)

    arrays = {
        "x": np.ascontiguousarray(x.reshape(B, C, H * W)),
        "norm_g": columns(inputs["L0_conv_norm_g"]),
        "norm_b": columns(inputs["L0_conv_norm_b"]),
        "qkv_wT": np.ascontiguousarray(np.asarray(inputs["L0_conv_qkv_w"]).T),
        "qkv_b": columns(inputs["L0_conv_qkv_b"]),
        "proj_wT": np.ascontiguousarray(np.asarray(inputs["L0_conv_proj_w"]).T),
        "proj_b": columns(inputs["L0_conv_proj_b"]),
    }
    nc = bacc.Bacc("TRN2", target_bir_lowering=False, num_devices=1)
    args = [nc.dram_tensor(n, a.shape, F32, kind="ExternalInput").ap() for n, a in arrays.items()]
    out = nc.dram_tensor("out", (B, C, H * W), F32, kind="ExternalOutput").ap()
    attention_block(nc, *args, out)
    result = run_bass_kernel_spmd(nc, [arrays], core_ids=[0])
    return result.results[0]["out"].reshape(B, C, H, W)
```

```python
from contextlib import ExitStack

import concourse.bass as bass
from concourse import mybir

F32 = mybir.dt.float32
F16 = mybir.dt.float16
ACT = mybir.ActivationFunctionType
ALU = mybir.AluOpType
AX = mybir.AxisListType

P = 128
HEADS = 8
GROUPS = 32
EPS = 1e-5
W_SCALE = 2.0 ** 8

STATS_STEPS = [1, 3, 5, 7, 9, 11, 13, 15]
NORMALISE_STEPS = [41, 42, 43, 44, 45, 46, 47, 48]
X_STEPS = [0, 0, 0, 0, 2, 4, 6, 8, 10, 12, 14, 16, 42, 43, 44, 45]
X_BUFS = 4

QKV = [("q", 0), ("k", 0), ("q", 1), ("k", 1), ("v", 0), ("v", 1)]


def begun(count):
    return not isinstance(count, int) or count > 0


def dense_schedule():
    steps = {1: [0, 2, 4, 6, 8, 10], 2: [16, 18, 20, 22, 24, 26], 3: [32, 34, 36, 38, 40, 42], 4: [46, 48, 50, 52, 56, 58]}
    out = [(t, kind, pair, part) for pair in steps for t, (kind, part) in zip(steps[pair], QKV)]
    out += [(t, "p", 0, part) for part, t in enumerate([12, 14, 17, 19, 21, 23, 28, 30])]
    out += [(t, "g", 0, part) for part, t in enumerate([25, 27])]
    return sorted(out)


def attention_block(nc, x, norm_g, norm_b, qkv_wT, qkv_b, proj_wT, proj_b, out):
    B, C, S = x.shape
    CT = C // P
    HD = C // HEADS
    ST = S // P
    HALF = S // 2
    NT = 2 * ST
    TB = NT * CT
    HB = TB // 8
    QKV_SCALE = 1.0 / W_SCALE
    ATT_SCALE = 1.0 / float(HD) ** 0.5
    assert (CT, HD, ST, NT) == (4, 64, 8, 16)

    DENSE = dense_schedule()
    PER_BATCH = len(DENSE)
    N_PROJ = 2 * CT
    BEFORE = [(0, "g", 0, 0), (0, "g", 0, 1)] + [(0, kind, 4, part) for kind, part in QKV]
    FIRST_DENSE = len(BEFORE)
    assert FIRST_DENSE == N_PROJ

    def dense_of(first, last):
        kept = [d for d in DENSE if not (first and d[1] == "p") and not (last and (d[1] == "g" or d[2] == 4))]
        return list(enumerate(kept))

    def dense_base(b):
        return FIRST_DENSE if isinstance(b, int) and b == 0 else b * PER_BATCH

    def place_of(first, last, kind, pair, part):
        return next(i for i, d in dense_of(first, last) if d[1:] == (kind, pair, part))

    with ExitStack() as ctx:
        def sb(name, shape, dt=F32):
            return ctx.enter_context(nc.sbuf_tensor(name, shape, dt))

        def psum(name, shape, dt=F32):
            return ctx.enter_context(nc.psum_tensor(name, shape, dt))

        def sem(name):
            return ctx.enter_context(nc.semaphore(name))

        w_qkv = sb("w_qkv", [P, 2, CT, 3 * C], F16)
        w_proj = sb("w_proj", [P, 2, CT, C], F16)
        x_in = sb("x_in", [P, X_BUFS, HALF])
        xn = sb("xn", [P, 2, CT, S], F16)
        qkv32 = sb("qkv32", [P, 2, HALF])
        q_nat = sb("q_nat", [P, 2, S], F16)
        k_nat = sb("k_nat", [P, 2, S], F16)
        q_st = sb("q_st", [P, 2, 2, S], F16)
        k_st = sb("k_st", [P, 2, 2, 2, S], F16)
        v_sb = sb("v_sb", [P, 2, ST, 2, P], F16)
        probs = sb("probs", [P, 2, S])
        pT = sb("pT", [P, 2, 2, ST, 2, HALF], F16)
        spread = sb("spread", [P, HALF // P, 2, HD])
        recip_rows = sb("recip_rows", [P, HALF])
        att32 = sb("att32", [P, HALF])
        att = sb("att", [P, 2, CT, S], F16)
        att_first = sb("att_first", [P, 2, S], F16)
        resid = sb("resid", [P, 2, HALF])
        out_sb = sb("out_sb", [P, 2, HALF])
        ident = sb("ident", [P, P])
        group_mean = sb("group_mean", [P, P])
        neg_max = sb("neg_max", [P, 4])
        row_sum = sb("row_sum", [P, 2, 8])
        recip = sb("recip", [P, 8])
        stats = sb("stats", [P, CT, 2, 6])
        mean_var = sb("mean_var", [P, CT, 2])
        g_mean = sb("g_mean", [P, CT])
        dev = sb("dev", [P, CT])
        dev2 = sb("dev2", [P, CT])
        c_var = sb("c_var", [P, CT])
        g_var = sb("g_var", [P, CT])
        rstd = sb("rstd", [P, CT])
        minus_half = sb("minus_half", [P, CT])
        xn_scale = sb("xn_scale", [P, CT])
        xn_shift = sb("xn_shift", [P, CT])
        mean_scaled = sb("mean_scaled", [P, CT])
        g_sb = sb("g_sb", [P, CT])
        b_sb = sb("b_sb", [P, CT])
        qkvb_sb = sb("qkvb_sb", [P, 3 * CT])
        qb_scaled = sb("qb_scaled", [P, CT])
        projb_sb = sb("projb_sb", [P, CT])
        w_in = pT[:].rearrange("p a b c d e -> p (a b c d e)").bitcast(F32)
        w_qkv_in = w_in[:, 0:CT * 3 * C].rearrange("p (c o) -> p c o", c=CT)
        att_in = att[:].rearrange("p a b c -> p (a b c)").bitcast(F32)
        w_proj_in = att_in[:, 0:CT * C].rearrange("p (c o) -> p c o", c=CT)

        scores = psum("scores", [P, 2, S])
        turned = psum("turned", [P, 2, HALF])
        att_acc = psum("att_acc", [P, HALF])
        dense = psum("dense", [P, HALF])

        small_in = sem("small_in")
        w_loaded = [sem(f"w_loaded{c}") for c in range(CT)]
        w_proj_loaded = sem("w_proj_loaded")
        x_loaded = [sem(f"x_loaded{n}") for n in range(X_BUFS)]
        const_steps = sem("const_steps")
        const_ready = sem("const_ready")
        bias_ready = sem("bias_ready")
        w_hi = sem("w_hi")
        w_ready = sem("w_ready")
        gn_done = sem("gn_done")
        rstd_ready = sem("rstd_ready")
        x_normal = sem("x_normal")
        xn_hi = sem("xn_hi")
        xn_lo = sem("xn_lo")
        dense_done = sem("dense_done")
        qkv_full = sem("qkv_full")
        qkv_hi = sem("qkv_hi")
        qkv_lo = sem("qkv_lo")
        q_stacked = sem("q_stacked")
        k_stacked = sem("k_stacked")
        scores_ready = sem("scores_ready")
        max_ready = sem("max_ready")
        probs_ready = sem("probs_ready")
        turned_ready = sem("turned_ready")
        pT_hi = sem("pT_hi")
        pT_lo = sem("pT_lo")
        recip_ready = sem("recip_ready")
        spread_ready = sem("spread_ready")
        rows_turned = sem("rows_turned")
        rows_ready = sem("rows_ready")
        att_done = sem("att_done")
        att_scaled = sem("att_scaled")
        att_biased = sem("att_biased")
        att_hi = sem("att_hi")
        att_lo = sem("att_lo")
        att_moved = sem("att_moved")
        proj_biased = sem("proj_biased")
        res_loaded = [sem("res_loaded0"), sem("res_loaded1")]
        out_ready = sem("out_ready")
        out_free = [sem("out_free0"), sem("out_free1")]

        def last_proj_bank(part):
            return dense[:, :] if part % 2 == 0 else scores[:, 0, 0:HALF]

        block = ctx.enter_context(nc.Block())

        def in_loop(engine, batch):
            batch(0, True, False)
            with engine.Fori(1, B - 1) as b:
                batch(b, False, False)
            batch(B - 1, False, True)

        @block.tensor
        def _(pe):
            def split_product(dst, w, r, n, count):
                for j, (i, k) in enumerate(((0, 0), (1, 0), (0, 1))):
                    last = nc.tensor.matmul(dst, w(i), r(k), start=n == 0 and j == 0, stop=n == count - 1 and j == 2)
                return last

            def wait_bank_left(b, before):
                _, kind, pair, part = before
                if kind == "p":
                    pe.wait_ge(proj_biased, N_PROJ * b - N_PROJ + part + 1)
                elif kind == "g":
                    pe.wait_ge(gn_done, 20 * b + (33, 37)[part])
                else:
                    pe.wait_ge(qkv_full, 24 * b + 6 * pair + QKV.index((kind, part)) + 1)

            def dense_chunk(b, chunk, bank):
                _, kind, pair, part = chunk
                h = pair % CT
                if kind == "g":
                    pe.wait_ge(gn_done, 20 * b + (32, 36)[part])
                    src = mean_var[:, :, 0] if part == 0 else c_var[:, :]
                    last = nc.tensor.matmul(bank[:, 0:CT], group_mean[:, :], src, start=True, stop=True)
                elif kind == "v":
                    for s in range(4):
                        k0 = (4 * part + s) * P
                        for c in range(CT):
                            last = split_product(bank[:, s * P:(s + 1) * P], lambda i: xn[:, i, c, k0:k0 + P],
                                                 lambda i: w_qkv[:, i, c, 2 * C + h * P:2 * C + (h + 1) * P], c, CT)
                elif kind == "p":
                    if part == 0:
                        pe.wait_ge(att_lo, HB * b)
                        pe.wait_ge(att_moved, 16 * b)
                        pe.wait_ge(w_ready, CT + 1)
                    o, n0 = part // 2, part % 2 * HALF
                    for c in range(CT):
                        last = split_product(bank, lambda i: w_proj[:, i, c, o * P:(o + 1) * P],
                                             lambda i: att[:, i, c, n0:n0 + HALF], c, CT)
                else:
                    if kind == "q" and pair == 4:
                        pe.wait_ge(xn_lo, 8 * b + 8 + 4 * (part + 1))
                    o = (0 if kind == "q" else C) + h * P
                    for c in range(CT):
                        last = split_product(bank, lambda i: w_qkv[:, i, c, o:o + P],
                                             lambda i: xn[:, i, c, part * HALF:(part + 1) * HALF], c, CT)
                last.then_inc(dense_done, 1)

            def score_tile(t):
                buf, head, q0 = t // NT % 2, t % 2, t % NT // 2 * P
                for bank in range(2):
                    for part in range(2):
                        last = nc.tensor.matmul(scores[:, t % 2, bank * HALF:(bank + 1) * HALF],
                                                q_st[:, buf, head, q0:q0 + P],
                                                k_st[:, buf, head, part, bank * HALF:(bank + 1) * HALF],
                                                start=part == 0, stop=part == 1)
                last.then_inc(scores_ready, 1)

            def attend(t, s):
                half = t // 8 - 1
                buf = half // 2 % 2
                for j, (i, k) in enumerate(((0, 0), (1, 0), (0, 1))):
                    for head in range(2):
                        last = nc.tensor.matmul(att_acc[head * HD:(head + 1) * HD, :],
                                                v_sb[:, buf, s, i, head * HD:(head + 1) * HD],
                                                pT[:, half % 2, k, s, head, :],
                                                start=s == 0 and j == 0, stop=s == ST - 1 and j == 2)
                if s == ST - 1:
                    last.then_inc(att_done, 1)

            def turn_rows():
                for q in range(HALF // P):
                    last = nc.tensor.transpose(turned[:, 0, q * P:(q + 1) * P],
                                               spread[:, q, :, :].rearrange("p h d -> p (h d)"), ident[:, :])
                last.then_inc(rows_turned, 1)

            def batch(b, first, final):
                for t in range(TB):
                    pe.wait_ge(probs_ready, TB * b + t + 1)
                    if not (final and t + 2 >= TB):
                        if (t + 2) % NT == 0:
                            pair = (t + 2) // NT
                            pe.wait_ge(q_stacked, 64 * CT * b + 64 * (pair + 1))
                            pe.wait_ge(k_stacked, 64 * CT * b + 64 * (pair + 1))
                        score_tile(t + 2)
                    for bank in range(2):
                        if begun(count := 2 * TB * b + 2 * t + bank - 1):
                            pe.wait_ge(pT_lo, count)
                        if t % 8 == 6 and bank == 0 and not (first and t < 8):
                            pe.wait_ge(rows_ready, HB * b + t // 8)
                        for s in range(4):
                            k0 = (4 * bank + s) * P
                            last = nc.tensor.transpose(turned[:, bank, s * P:(s + 1) * P],
                                                       probs[:, t % 2, k0:k0 + P], ident[:, :])
                        last.then_inc(turned_ready, 1)
                    for i, chunk in dense_of(first, final):
                        if chunk[0] == t:
                            if i == 0:
                                wait_bank_left(b - 1, BEFORE[-1])
                            else:
                                wait_bank_left(b, dense_of(first, final)[i - 1][1])
                            dense_chunk(b, chunk, dense[:, :])
                    if not (first and t < 8):
                        dense_steps = [chunk[0] for _, chunk in dense_of(first, final)]
                        s = t % 8
                        if t // 2 * 2 in dense_steps:
                            blocks = [s - 1, s] if t % 2 else []
                        else:
                            blocks = [s]
                        if 0 in blocks:
                            pe.wait_ge(pT_lo, 2 * TB * b + 2 * (t - s))
                            if begun(count := HB * b + t // 8 - 1):
                                pe.wait_ge(att_scaled, count)
                            if t % NT >= 8:
                                pe.wait_ge(qkv_lo, 24 * b + 6 * (t // NT) + 6)
                        for block_of_keys in blocks:
                            attend(t, block_of_keys)
                        if t % 8 == 5:
                            pe.wait_ge(spread_ready, HB * b + t // 8)
                            pe.wait_ge(pT_lo, 2 * TB * b + 2 * t + 1)
                            turn_rows()

            pe.wait_ge(const_ready, 1)
            for i, chunk in enumerate(BEFORE):
                if i == 2:
                    pe.wait_ge(w_ready, CT)
                if i:
                    wait_bank_left(-1, BEFORE[i - 1])
                dense_chunk(-1, chunk, dense[:, :])
            pe.wait_ge(q_stacked, 64)
            pe.wait_ge(k_stacked, 64)
            score_tile(0)
            score_tile(1)
            in_loop(pe, batch)
            pe.wait_ge(pT_lo, 2 * TB * B)
            pe.wait_ge(att_scaled, HB * B - 1)
            for s in range(ST):
                attend(TB, s)
            pe.wait_ge(spread_ready, HB * B)
            turn_rows()
            for part in range(N_PROJ):
                if part == 0:
                    wait_bank_left(B - 1, dense_of(False, True)[-1][1])
                elif part >= 2:
                    pe.wait_ge(proj_biased, N_PROJ * (B - 1) + part - 1)
                dense_chunk(B, (0, "p", 0, part), last_proj_bank(part))

        @block.scalar
        def _(act):
            def drain_dense(b, number, chunk, bank=dense):
                _, kind, pair, part = chunk
                if kind == "g":
                    return
                h = pair % CT
                act.wait_ge(dense_done, number + 1)
                if kind == "p":
                    act.wait_ge(out_free[part % 2], 64 * b - 48 + 16 * (part // 2))
                    nc.scalar.activation(out_sb[:, part % 2, :], bank[:, :], ACT.Identity,
                                         bias=projb_sb[:, part // 2:part // 2 + 1], scale=QKV_SCALE)\
                        .then_inc(proj_biased, 1)
                    return
                n = QKV.index((kind, part))
                if begun(count := 24 * b + 6 * pair + n - 1):
                    act.wait_ge(qkv_lo, count)
                if kind == "q":
                    scale, bias = QKV_SCALE * ATT_SCALE, qb_scaled[:, h:h + 1]
                elif kind == "k":
                    scale, bias = QKV_SCALE, qkvb_sb[:, CT + h:CT + h + 1]
                else:
                    scale, bias = QKV_SCALE, 0.0
                nc.scalar.activation(qkv32[:, n % 2, :], bank[:, :], ACT.Identity, bias=bias, scale=scale)\
                    .then_inc(qkv_full, 1)

            def normal_hi(b, n):
                c, part = n % CT, n // CT
                act.wait_ge(x_normal, 8 * b + 8 + n + 1)
                nc.scalar.activation(xn[:, 0, c, part * HALF:(part + 1) * HALF], x_in[:, n % X_BUFS, :], ACT.Copy)\
                    .then_inc(xn_hi, 1)

            def exp_tile(b, t):
                act.wait_ge(max_ready, TB * b + t + 1)
                if t % 8 == 0:
                    if begun(count := HB * b + t // 8 - 1):
                        act.wait_ge(recip_ready, count)
                nc.scalar.activation(probs[:, t % 2, :], scores[:, t % 2, :], ACT.Exp,
                                     bias=neg_max[:, t % 4:t % 4 + 1],
                                     accum_out=row_sum[:, t // 8 % 2, t % 8:t % 8 + 1]).then_inc(probs_ready, 1)

            def turned_hi(b, t, bank):
                act.wait_ge(turned_ready, 2 * TB * b + 2 * t + bank + 1)
                if t % 8 == 0 and bank == 0:
                    if begun(count := HB * b + t // 8 - 1):
                        act.wait_ge(att_done, count)
                q0 = t % 8 // 2 * P
                nc.scalar.activation(pT[:, t // 8 % 2, 0, 4 * bank:4 * bank + 4, t % 2, q0:q0 + P],
                                     turned[:, bank, :].rearrange("p (s q) -> p s q", q=P), ACT.Copy).then_inc(pT_hi, 1)

            def spread_recip(b, half):
                act.wait_ge(recip_ready, HB * b + half + 1)
                if begun(count := HB * b + half):
                    act.wait_ge(rows_turned, count)
                nc.scalar.activation(spread[:, :, :, :].rearrange("p q h d -> p (q h) d"),
                                     recip[:, :].unsqueeze(2).to_broadcast([P, 8, HD]), ACT.Copy).then_inc(spread_ready, 1)

            def keep_rows(b, half):
                act.wait_ge(rows_turned, HB * b + half + 1)
                if begun(count := HB * b + half):
                    act.wait_ge(att_scaled, count)
                nc.scalar.activation(recip_rows[:, :], turned[:, 0, :], ACT.Copy).then_inc(rows_ready, 1)

            def batch(b, first, final):
                for t in range(TB):
                    if t % 8 == 6 and not (first and t < 8):
                        keep_rows(b, t // 8 - 1)
                    for bank in range(2):
                        turned_hi(b, t, bank)
                    if not (final and t + 2 >= TB):
                        exp_tile(b, t + 2)
                    for i, chunk in dense_of(first, final):
                        if chunk[0] == t:
                            drain_dense(b, dense_base(b) + i, chunk)
                    if t % 8 == 2 and not (first and t < 8):
                        spread_recip(b, t // 8 - 1)
                    if not final and t in NORMALISE_STEPS:
                        n = NORMALISE_STEPS.index(t)
                        if n % CT == 0:
                            act.wait_ge(dense_done, dense_base(b) + place_of(first, final, "v", 3, n // CT) + 1)
                        normal_hi(b, n)
                    if first and t == 8:
                        act.wait_ge(w_proj_loaded, 16)
                        nc.scalar.activation(w_proj[:, 0, :, :], w_proj_in, ACT.Copy, scale=W_SCALE).then_inc(w_hi, 1)

            act.wait_ge(small_in, 48)
            act.wait_ge(out_free[0], 16)
            act.wait_ge(out_free[1], 16)
            nc.scalar.mul(qb_scaled[:, :], qkvb_sb[:, 0:CT], ATT_SCALE).then_inc(bias_ready, 1)
            for c in range(CT):
                act.wait_ge(w_loaded[c], 16)
                nc.scalar.activation(w_qkv[:, 0, c, :], w_qkv_in[:, c, :], ACT.Copy, scale=W_SCALE).then_inc(w_hi, 1)
            for n in range(2 * CT):
                normal_hi(-1, n)
            act.wait_ge(bias_ready, 1)
            for i, chunk in enumerate(BEFORE):
                drain_dense(-1, i, chunk)
            exp_tile(0, 0)
            exp_tile(0, 1)
            in_loop(act, batch)
            spread_recip(B - 1, HB - 1)
            keep_rows(B - 1, HB - 1)
            base = PER_BATCH * (B - 1) + len(dense_of(False, True))
            for part in range(N_PROJ):
                drain_dense(B, base + part, (0, "p", 0, part), last_proj_bank(part))

        @block.vector
        def _(dve):
            def gn_stats(b, n):
                buf = n % X_BUFS
                dve.wait_ge(x_loaded[buf], 64 * b + 80 + 16 * (n // X_BUFS))
                nc.vector.bn_stats(stats[:, n // 2, n % 2, :], x_in[:, buf, :]).then_inc(gn_done, 1)

            def gn_aggregate(c):
                nc.vector.bn_aggr(mean_var[:, c, :], stats[:, c, :, :]).then_inc(gn_done, 1)

            def gn_mean(b, number):
                n0 = 20 * b + 20
                dve.wait_ge(dense_done, number + 1)
                nc.vector.tensor_copy(g_mean[:, :], dense[:, 0:CT]).then_inc(gn_done, 1)
                dve.wait_ge(gn_done, n0 + 13)
                nc.vector.tensor_tensor(dev[:, :], mean_var[:, :, 0], g_mean[:, :], ALU.subtract).then_inc(gn_done, 1)
                dve.wait_ge(gn_done, n0 + 14)
                nc.vector.tensor_tensor(dev2[:, :], dev[:, :], dev[:, :], ALU.mult).then_inc(gn_done, 1)
                dve.wait_ge(gn_done, n0 + 15)
                nc.vector.tensor_tensor(c_var[:, :], dev2[:, :], mean_var[:, :, 1], ALU.add).then_inc(gn_done, 1)

            def gn_affine(b, number):
                n0 = 20 * b + 20
                dve.wait_ge(dense_done, number + 1)
                nc.vector.tensor_scalar(g_var[:, :], dense[:, 0:CT], EPS, None, ALU.add)\
                    .then_inc(gn_done, 1)
                dve.wait_ge(rstd_ready, b + 2)
                nc.vector.tensor_tensor(xn_scale[:, :], rstd[:, :], g_sb[:, :], ALU.mult).then_inc(gn_done, 1)
                dve.wait_ge(gn_done, n0 + 18)
                nc.vector.tensor_tensor(mean_scaled[:, :], g_mean[:, :], xn_scale[:, :], ALU.mult).then_inc(gn_done, 1)
                dve.wait_ge(gn_done, n0 + 19)
                nc.vector.tensor_tensor(xn_shift[:, :], b_sb[:, :], mean_scaled[:, :], ALU.subtract).then_inc(gn_done, 1)

            def max_tile(b, t):
                dve.wait_ge(scores_ready, TB * b + t + 1)
                nc.vector.tensor_reduce(neg_max[:, t % 4:t % 4 + 1], scores[:, t % 2, :], AX.X, ALU.max,
                                        negate=True).then_inc(max_ready, 1)

            def turned_lo(b, t, bank):
                dve.wait_ge(pT_hi, 2 * TB * b + 2 * t + bank + 1)
                q0 = t % 8 // 2 * P
                part = [pT[:, t // 8 % 2, i, 4 * bank:4 * bank + 4, t % 2, q0:q0 + P] for i in range(2)]
                nc.vector.tensor_tensor(part[1], turned[:, bank, :].rearrange("p (s q) -> p s q", q=P), part[0],
                                        ALU.subtract).then_inc(pT_lo, 1)

            def scale_att(b, half):
                dve.wait_ge(att_done, HB * b + half + 1)
                dve.wait_ge(rows_ready, HB * b + half + 1)
                if begun(count := HB * b + half):
                    dve.wait_ge(att_lo, count)
                nc.vector.tensor_tensor(att32[:, :], att_acc[:, :], recip_rows[:, :], ALU.mult).then_inc(att_scaled, 1)

            def bias_att(b, half):
                pair = half // 2
                dve.wait_ge(att_scaled, HB * b + half + 1)
                nc.vector.tensor_scalar(att32[:, :], att32[:, :], qkvb_sb[:, 2 * CT + pair:2 * CT + pair + 1], None,
                                        ALU.add).then_inc(att_biased, 1)

            def att_split_hi(b, half, att_read=0):
                pair, n0 = half // 2, half % 2 * HALF
                dve.wait_ge(att_biased, HB * b + half + 1)
                if half == 0 and begun(count := 16 * b):
                    dve.wait_ge(att_moved, count)
                if begun(att_read):
                    dve.wait_ge(dense_done, att_read)
                dst = att_first[:, 0, n0:n0 + HALF] if pair == 0 else att[:, 0, pair, n0:n0 + HALF]
                nc.vector.tensor_copy(dst, att32[:, :]).then_inc(att_hi, 1)

            def qkv_split_hi(b, chunk):
                _, kind, pair, part = chunk
                n = QKV.index((kind, part))
                dve.wait_ge(qkv_full, 24 * b + 6 * pair + n + 1)
                if kind == "v":
                    if begun(count := HB * b + 2 * pair - 2):
                        dve.wait_ge(att_done, count)
                    full = qkv32[:, n % 2, :].rearrange("p (s c) -> p s c", c=P)
                    hi = v_sb[:, pair % 2, 4 * part:4 * part + 4, 0, :]
                else:
                    nat, stacked = (q_nat, q_stacked) if kind == "q" else (k_nat, k_stacked)
                    if begun(count := 64 * CT * b + 64 * pair):
                        dve.wait_ge(stacked, count)
                    full, hi = qkv32[:, n % 2, :], nat[:, 0, part * HALF:(part + 1) * HALF]
                nc.vector.tensor_copy(hi, full).then_inc(qkv_hi, 1)

            def normalise(b, n):
                c, part, buf = n % CT, n // CT, n % X_BUFS
                dve.wait_ge(x_loaded[buf], 64 * b + 112 + 16 * part)
                dve.wait_ge(gn_done, 20 * b + 40)
                nc.vector.tensor_scalar(x_in[:, buf, :], x_in[:, buf, :], xn_scale[:, c:c + 1], xn_shift[:, c:c + 1],
                                        ALU.mult, ALU.add).then_inc(x_normal, 1)

            def invert_sums(b, half):
                dve.wait_ge(probs_ready, TB * b + 8 * half + 8)
                if begun(count := HB * b + half):
                    dve.wait_ge(spread_ready, count)
                nc.vector.reciprocal(recip[:, :], row_sum[:, half % 2, :]).then_inc(recip_ready, 1)

            def batch(b, first, final):
                for t in range(TB):
                    if t % 8 == 0 and not (first and t < 16):
                        if t >= 16:
                            scale_att(b, t // 8 - 2)
                        else:
                            scale_att(b - 1, HB - 2 + t // 8)
                    aggregate = not final and t - 1 in STATS_STEPS[1::2]
                    if aggregate:
                        c = STATS_STEPS.index(t - 1) // 2
                        dve.wait_ge(gn_done, 20 * b + 20 + 3 * c + 2)
                    if not (final and t + 2 >= TB):
                        max_tile(b, t + 2)
                    if aggregate:
                        gn_aggregate(c)
                    for bank in range(2):
                        turned_lo(b, t, bank)
                    if t % 8 in (0, 1) and not (first and t < 16):
                        at_batch, half = (b, t // 8 - 2) if t >= 16 else (b - 1, HB - 2 + t // 8)
                        if t % 8 == 0:
                            bias_att(at_batch, half)
                        elif t == 33 and not first:
                            att_split_hi(b, 2, dense_base(b) + place_of(first, final, "p", 0, 7) + 1)
                        else:
                            att_split_hi(at_batch, half)
                    for i, chunk in dense_of(first, final):
                        if chunk[0] + 1 == t and chunk[1] in "qkv":
                            qkv_split_hi(b, chunk)
                    if not final and t in NORMALISE_STEPS:
                        normalise(b, NORMALISE_STEPS.index(t))
                    if t % 8 == 0 and not (first and t < 8):
                        if t >= 8:
                            invert_sums(b, t // 8 - 1)
                        else:
                            invert_sums(b - 1, HB - 1)
                    if not final and t in STATS_STEPS:
                        gn_stats(b, STATS_STEPS.index(t))
                    for i, chunk in dense_of(first, final):
                        if chunk[0] == t and chunk[1] == "g":
                            (gn_mean, gn_affine)[chunk[3]](b, dense_base(b) + i)
                    if first and t == 9:
                        dve.wait_ge(w_hi, CT + 1)
                        nc.vector.scalar_tensor_tensor(w_proj[:, 1, :, :], w_proj_in, W_SCALE, w_proj[:, 0, :, :],
                                                       ALU.mult, ALU.subtract).then_inc(w_ready, 1)

            for n in range(2 * CT):
                gn_stats(-1, n)
                if n % 2:
                    dve.wait_ge(gn_done, 3 * (n // 2) + 2)
                    gn_aggregate(n // 2)
            dve.wait_ge(small_in, 48)
            gn_mean(-1, 0)
            gn_affine(-1, 1)
            for n in range(2 * CT):
                normalise(-1, n)
            for c in range(CT):
                dve.wait_ge(w_hi, c + 1)
                nc.vector.scalar_tensor_tensor(w_qkv[:, 1, c, :], w_qkv_in[:, c, :], W_SCALE, w_qkv[:, 0, c, :],
                                               ALU.mult, ALU.subtract).then_inc(w_ready, 1)
            for chunk in BEFORE[2:]:
                qkv_split_hi(-1, chunk)
            max_tile(0, 0)
            max_tile(0, 1)
            in_loop(dve, batch)
            scale_att(B - 1, HB - 2)
            invert_sums(B - 1, HB - 1)
            bias_att(B - 1, HB - 2)
            att_split_hi(B - 1, HB - 2)
            scale_att(B - 1, HB - 1)
            bias_att(B - 1, HB - 1)
            att_split_hi(B - 1, HB - 1)

        @block.gpsimd
        def _(pool):
            def qkv_split_lo(b, chunk):
                _, kind, pair, part = chunk
                n = QKV.index((kind, part))
                pool.wait_ge(qkv_hi, 24 * b + 6 * pair + n + 1)
                if kind == "v":
                    full = qkv32[:, n % 2, :].rearrange("p (s c) -> p s c", c=P)
                    hi, lo = (v_sb[:, pair % 2, 4 * part:4 * part + 4, i, :] for i in range(2))
                else:
                    nat = q_nat if kind == "q" else k_nat
                    full = qkv32[:, n % 2, :]
                    hi, lo = (nat[:, i, part * HALF:(part + 1) * HALF] for i in range(2))
                nc.gpsimd.tensor_tensor(lo, full, hi, ALU.subtract).then_inc(qkv_lo, 1)

            def xn_split_lo(b, n):
                c, at = n % CT, slice(n // CT * HALF, (n // CT + 1) * HALF)
                pool.wait_ge(xn_hi, 8 * b + 8 + n + 1)
                nc.gpsimd.tensor_tensor(xn[:, 1, c, at], x_in[:, n % X_BUFS, :], xn[:, 0, c, at], ALU.subtract)\
                    .then_inc(xn_lo, 1)

            def att_split_lo(b, half):
                pair, n0 = half // 2, half % 2 * HALF
                pool.wait_ge(att_hi, HB * b + half + 1)
                hi, lo = ((att_first[:, i, n0:n0 + HALF] if pair == 0 else att[:, i, pair, n0:n0 + HALF]) for i in range(2))
                nc.gpsimd.tensor_tensor(lo, att32[:, :], hi, ALU.subtract).then_inc(att_lo, 1)

            def add_residual(b, part):
                pool.wait_ge(res_loaded[part % 2], 64 * b - 64 + 16 * (part // 2) + 16)
                pool.wait_ge(proj_biased, N_PROJ * b - N_PROJ + part + 1)
                nc.gpsimd.tensor_tensor(out_sb[:, part % 2, :], out_sb[:, part % 2, :], resid[:, part % 2, :], ALU.add)\
                    .then_inc(out_ready, 1)

            def invert_std(b):
                pool.wait_ge(gn_done, 20 * b + 37)
                nc.gpsimd.tensor_tensor(rstd[:, :], g_var[:, :], minus_half[:, :], ALU.pow).then_inc(rstd_ready, 1)

            def batch(b, first, final):
                for t in range(TB):
                    for i, chunk in dense_of(first, final):
                        if chunk[0] + 1 == t and chunk[1] in "qkv":
                            qkv_split_lo(b, chunk)
                        if chunk[0] == t:
                            if chunk[1] == "p":
                                add_residual(b, chunk[3])
                            elif chunk[1] == "g" and chunk[3] == 1:
                                invert_std(b)
                    if t % 8 == 1 and not (first and t < 16):
                        if t >= 16:
                            att_split_lo(b, t // 8 - 2)
                        else:
                            att_split_lo(b - 1, HB - 2 + t // 8)
                    if not final and t in NORMALISE_STEPS:
                        xn_split_lo(b, NORMALISE_STEPS.index(t))

            nc.gpsimd.memset(ident[:, :], 0.0).then_inc(const_steps, 1)
            nc.gpsimd.memset(group_mean[:, :], GROUPS / C).then_inc(const_steps, 1)
            nc.gpsimd.memset(minus_half[:, :], -0.5).then_inc(const_steps, 1)
            pool.wait_ge(const_steps, 3)
            nc.gpsimd.affine_select(out=ident[:, :], in_=ident[:, :], compare_op=ALU.not_equal, fill=1.0, base=0,
                                    pattern=[[-1, P]], channel_multiplier=1).then_inc(const_steps, 1)
            per = C // GROUPS
            blocks = group_mean[:, :].rearrange("p (g c) -> p g c", c=per)
            nc.gpsimd.affine_select(out=blocks, in_=blocks, compare_op=ALU.is_ge, fill=0.0, base=0,
                                    pattern=[[-per, P // per], [0, per]], channel_multiplier=1).then_inc(const_steps, 1)
            pool.wait_ge(const_steps, 5)
            nc.gpsimd.affine_select(out=blocks, in_=blocks, compare_op=ALU.is_ge, fill=0.0, base=per - 1,
                                    pattern=[[per, P // per], [0, per]], channel_multiplier=-1).then_inc(const_ready, 1)
            invert_std(-1)
            for n in range(2 * CT):
                xn_split_lo(-1, n)
            for chunk in BEFORE[2:]:
                qkv_split_lo(-1, chunk)
            in_loop(pool, batch)
            att_split_lo(B - 1, HB - 2)
            att_split_lo(B - 1, HB - 1)
            for part in range(N_PROJ):
                add_residual(B, part)

        @block.sync
        def _(sp):
            def row(ap, b):
                return ap[bass.ds(b, 1)].rearrange("o c s -> (o c) s")

            def load_x(b, k):
                buf = k % X_BUFS
                c, part = (k // 2, k % 2) if k < 8 else (k % CT, (k - 8) // CT)
                if k < 4:
                    if begun(count := 8 * b + 5 + k):
                        sp.wait_ge(xn_lo, count)
                elif k < 12:
                    sp.wait_ge(gn_done, 20 * b + 20 + 3 * ((k - 4) // 2) + 1 + (k - 4) % 2)
                else:
                    sp.wait_ge(xn_lo, 8 * b + 8 + k - 11)
                sp.dma_start(x_in[:, buf, :], row(x, b + 1)[c * P:(c + 1) * P, part * HALF:(part + 1) * HALF])\
                    .then_inc(x_loaded[buf], 16)

            def stack_q(b, pair):
                buf, h = pair % 2, HD
                sp.wait_ge(qkv_lo, 24 * b + 6 * pair + 3)
                for dst, head, src, part in ((0, 0, 0, 0), (h, 0, 0, 1), (0, 1, h, 1), (h, 1, h, 0)):
                    sp.dma_start(q_st[dst:dst + h, buf, head, :], q_nat[src:src + h, part, :]).then_inc(q_stacked, 16)

            def stack_k(b, pair):
                buf, h = pair % 2, HD
                sp.wait_ge(qkv_lo, 24 * b + 6 * pair + 4)
                for head in range(2):
                    for dst in (0, h):
                        sp.dma_start(k_st[dst:dst + h, buf, head, :, :], k_nat[head * h:(head + 1) * h, :, :])\
                            .then_inc(k_stacked, 16)

            def load_residual(b, part):
                o, n0 = part // 2, part % 2 * HALF
                if part < 2:
                    sp.wait_ge(out_free[part], 64 * b - 48)
                else:
                    sp.wait_ge(out_ready, N_PROJ * b - N_PROJ + part - 1)
                sp.dma_start(resid[:, part % 2, :], row(x, b - 1)[o * P:(o + 1) * P, n0:n0 + HALF])\
                    .then_inc(res_loaded[part % 2], 16)

            def store(b, part):
                o, n0 = part // 2, part % 2 * HALF
                sp.wait_ge(out_ready, N_PROJ * b - N_PROJ + part + 1)
                sp.dma_start(row(out, b - 1)[o * P:(o + 1) * P, n0:n0 + HALF], out_sb[:, part % 2, :])\
                    .then_inc(out_free[part % 2], 16)

            def move_first(b, first, final):
                sp.wait_ge(att_lo, HB * b + 2)
                if not first:
                    sp.wait_ge(dense_done, dense_base(b) + place_of(first, final, "p", 0, 7) + 1)
                sp.dma_start(att[:, :, 0, :], att_first[:, :, :]).then_inc(att_moved, 16)

            def batch(b, first, final):
                for t in range(TB):
                    for i, chunk in dense_of(first, final):
                        at, kind, pair, part = chunk
                        if at + 2 == t and kind in "qk" and part == 1:
                            (stack_q if kind == "q" else stack_k)(b, pair)
                        if at + 1 == t and kind == "p":
                            store(b, part)
                        if at - 1 == t and kind == "p":
                            load_residual(b, part)
                    if not final and t in X_STEPS:
                        for k in [k for k, s in enumerate(X_STEPS) if s == t]:
                            load_x(b, k)
                    if t == 33:
                        move_first(b, first, final)

            for k in range(X_BUFS):
                load_x(-1, k)
            for dst, src in ((g_sb, norm_g), (b_sb, norm_b), (qkvb_sb, qkv_b)):
                sp.dma_start(dst[:, :], src).then_inc(small_in, 16)
            for n in range(2):
                cols = slice(n * CT // 2, (n + 1) * CT // 2)
                sp.dma_start(projb_sb[:, cols], proj_b[:, cols]).then_inc(out_free[n], 16)
            for k in range(X_BUFS, 3 * X_BUFS):
                load_x(-1, k)
                if k % 2:
                    c = (k - X_BUFS) // 2
                    sp.dma_start(w_qkv_in[:, c, :], qkv_wT[c * P:(c + 1) * P, :]).then_inc(w_loaded[c], 16)
            for k in range(3 * X_BUFS, 4 * X_BUFS):
                load_x(-1, k)
            sp.dma_start(w_proj_in, proj_wT.rearrange("(c p) o -> p c o", p=P)).then_inc(w_proj_loaded, 16)
            stack_q(-1, 4)
            stack_k(-1, 4)
            in_loop(sp, batch)
            for part in range(2):
                load_residual(B, part)
            for part in range(N_PROJ):
                store(B, part)
                if part + 2 < N_PROJ:
                    load_residual(B, part + 2)
            for buf in range(2):
                sp.wait_ge(out_free[buf], 16 + 64 * B)


def kernel(**inputs):
    import numpy as np
    import concourse.bacc as bacc
    from concourse.bass_utils import run_bass_kernel_spmd

    x = np.asarray(inputs["x"])
    B, C, H, W = x.shape

    def columns(v):
        return np.ascontiguousarray(np.asarray(v).reshape(-1, P).T)

    arrays = {
        "x": np.ascontiguousarray(x.reshape(B, C, H * W)),
        "norm_g": columns(inputs["L0_conv_norm_g"]),
        "norm_b": columns(inputs["L0_conv_norm_b"]),
        "qkv_wT": np.ascontiguousarray(np.asarray(inputs["L0_conv_qkv_w"]).T),
        "qkv_b": columns(inputs["L0_conv_qkv_b"]),
        "proj_wT": np.ascontiguousarray(np.asarray(inputs["L0_conv_proj_w"]).T),
        "proj_b": columns(inputs["L0_conv_proj_b"]),
    }
    nc = bacc.Bacc("TRN2", target_bir_lowering=False, num_devices=1)
    args = [nc.dram_tensor(n, a.shape, F32, kind="ExternalInput").ap() for n, a in arrays.items()]
    out = nc.dram_tensor("out", (B, C, H * W), F32, kind="ExternalOutput").ap()
    attention_block(nc, *args, out)
    result = run_bass_kernel_spmd(nc, [arrays], core_ids=[0])
    return result.results[0]["out"].reshape(B, C, H, W)
```

```python
from contextlib import ExitStack

import concourse.bass as bass
from concourse import mybir

F32 = mybir.dt.float32
F16 = mybir.dt.float16
ACT = mybir.ActivationFunctionType
ALU = mybir.AluOpType
AX = mybir.AxisListType

P = 128
HEADS = 8
GROUPS = 32
EPS = 1e-5
W_SCALE = 2.0 ** 8

STATS_STEPS = [1, 3, 5, 7, 9, 11, 13, 15]
NORMALISE_STEPS = [40, 41, 42, 43, 46, 47, 48, 49]
X_STEPS = [0, 0, 0, 0, 2, 4, 6, 8, 10, 12, 14, 16, 42, 43, 44, 45]
X_BUFS = 4

QKV = [("q", 0), ("k", 0), ("q", 1), ("k", 1), ("v", 0), ("v", 1)]


def begun(count):
    return not isinstance(count, int) or count > 0


def is_batch(b, number):
    return isinstance(b, int) and b == number


def dense_schedule():
    steps = {1: [0, 2, 4, 6, 8, 10], 2: [16, 18, 20, 22, 24, 26], 3: [32, 34, 36, 38, 40, 42], 4: [46, 48, 52, 56, 58, 62]}
    out = [(t, kind, pair, part) for pair in steps for t, (kind, part) in zip(steps[pair], QKV)]
    out += [(t, "p", 0, part) for part, t in enumerate([12, 14, 17, 21, 23, 28, 29, 30])]
    out += [(t, "g", 0, part) for part, t in enumerate([25, 31])]
    return sorted(out)


def attention_block(nc, x, norm_g, norm_b, qkv_wT, qkv_b, proj_wT, proj_b, out):
    B, C, S = x.shape
    CT = C // P
    HD = C // HEADS
    ST = S // P
    HALF = S // 2
    NT = 2 * ST
    TB = NT * CT
    HB = TB // 8
    QKV_SCALE = 1.0 / W_SCALE
    ATT_SCALE = 1.0 / float(HD) ** 0.5
    assert (CT, HD, ST, NT) == (4, 64, 8, 16)

    DENSE = dense_schedule()
    PER_BATCH = len(DENSE)
    N_PROJ = 2 * CT
    BEFORE = [(0, "g", 0, 0), (0, "g", 0, 1)] + [(0, kind, 4, part) for kind, part in QKV]
    FIRST_DENSE = len(BEFORE)
    assert FIRST_DENSE == N_PROJ

    def dense_of(first, last):
        kept = [d for d in DENSE if not (first and d[1] == "p") and not (last and (d[1] == "g" or d[2] == 4))]
        return list(enumerate(kept))

    def dense_base(b):
        return FIRST_DENSE if is_batch(b, 0) else b * PER_BATCH

    def place_of(first, last, kind, pair, part):
        return next(i for i, d in dense_of(first, last) if d[1:] == (kind, pair, part))

    with ExitStack() as ctx:
        def sb(name, shape, dt=F32):
            return ctx.enter_context(nc.sbuf_tensor(name, shape, dt))

        def psum(name, shape, dt=F32):
            return ctx.enter_context(nc.psum_tensor(name, shape, dt))

        def sem(name):
            return ctx.enter_context(nc.semaphore(name))

        w_qkv = sb("w_qkv", [P, 2, CT, 3 * C], F16)
        w_proj = sb("w_proj", [P, 2, CT, C], F16)
        x_in = sb("x_in", [P, X_BUFS, HALF])
        xn = sb("xn", [P, 2, CT, S], F16)
        qkv32 = sb("qkv32", [P, 2, HALF])
        q_nat = sb("q_nat", [P, 2, S], F16)
        k_nat = sb("k_nat", [P, 2, S], F16)
        q_st = sb("q_st", [P, 2, 2, S], F16)
        k_st = sb("k_st", [P, 2, 2, 2, S], F16)
        v_sb = sb("v_sb", [P, 2, ST, 2, P], F16)
        probs = sb("probs", [P, 2, S])
        pT = sb("pT", [P, 2, 2, ST, 2, HALF], F16)
        recip_turned = sb("recip_turned", [8, P])
        recip_rows = sb("recip_rows", [P, HALF])
        att32 = sb("att32", [P, HALF])
        att = sb("att", [P, 2, CT, S], F16)
        att_first = sb("att_first", [P, 2, S], F16)
        resid = sb("resid", [P, 2, HALF])
        out_sb = sb("out_sb", [P, 2, HALF])
        ident = sb("ident", [P, P])
        group_mean = sb("group_mean", [P, P])
        neg_max = sb("neg_max", [P, 4])
        row_sum = sb("row_sum", [P, 2, 8])
        recip = sb("recip", [P, 8])
        stats = sb("stats", [P, CT, 2, 6])
        mean_var = sb("mean_var", [P, CT, 2])
        g_mean = sb("g_mean", [P, CT])
        dev = sb("dev", [P, CT])
        dev2 = sb("dev2", [P, CT])
        c_var = sb("c_var", [P, CT])
        g_var = sb("g_var", [P, CT])
        rstd = sb("rstd", [P, CT])
        minus_half = sb("minus_half", [P, CT])
        xn_scale = sb("xn_scale", [P, CT])
        xn_shift = sb("xn_shift", [P, CT])
        mean_scaled = sb("mean_scaled", [P, CT])
        g_sb = sb("g_sb", [P, CT])
        b_sb = sb("b_sb", [P, CT])
        qkvb_sb = sb("qkvb_sb", [P, 3 * CT])
        qb_scaled = sb("qb_scaled", [P, CT])
        projb_sb = sb("projb_sb", [P, CT])
        pT_start = [pT[:, n].rearrange("p b c d e -> p (b c d e)").bitcast(F32) for n in range(2)]
        x_first = pT_start[0][:, 0:CT * S].rearrange("p (c s) -> p c s", c=CT)
        w_qkv_in = pT_start[1][:, 0:CT * 3 * C].rearrange("p (c o) -> p c o", c=CT)
        att_in = att[:].rearrange("p a b c -> p (a b c)").bitcast(F32)
        w_proj_in = att_in[:, 0:CT * C].rearrange("p (c o) -> p c o", c=CT)

        recip_dram = nc.dram_tensor("recip_dram", (8, P), F32, kind="Internal").ap()

        scores = psum("scores", [P, 2, S])
        turned = psum("turned", [P, 2, HALF])
        att_acc = psum("att_acc", [P, HALF])
        dense = psum("dense", [P, HALF])

        small_in = sem("small_in")
        w_loaded = [sem(f"w_loaded{n}") for n in range(6)]
        w_proj_loaded = sem("w_proj_loaded")
        x_loaded = [sem(f"x_loaded{n}") for n in range(X_BUFS)]
        const_steps = sem("const_steps")
        const_ready = sem("const_ready")
        bias_ready = sem("bias_ready")
        w_hi = sem("w_hi")
        w_ready = sem("w_ready")
        gn_done = sem("gn_done")
        rstd_ready = sem("rstd_ready")
        x_normal = sem("x_normal")
        xn_hi = sem("xn_hi")
        xn_lo = sem("xn_lo")
        dense_done = sem("dense_done")
        qkv_full = sem("qkv_full")
        qkv_hi = sem("qkv_hi")
        qkv_lo = sem("qkv_lo")
        q_stacked = sem("q_stacked")
        k_stacked = sem("k_stacked")
        scores_ready = sem("scores_ready")
        max_ready = sem("max_ready")
        probs_ready = sem("probs_ready")
        turned_ready = sem("turned_ready")
        pT_hi = sem("pT_hi")
        pT_lo = sem("pT_lo")
        recip_ready = sem("recip_ready")
        rows_turned = sem("rows_turned")
        rows_kept = sem("rows_kept")
        rows_out = sem("rows_out")
        rows_in = sem("rows_in")
        att_done = sem("att_done")
        att_scaled = sem("att_scaled")
        att_biased = sem("att_biased")
        att_hi = sem("att_hi")
        att_lo = sem("att_lo")
        att_moved = sem("att_moved")
        proj_biased = sem("proj_biased")
        res_loaded = [sem("res_loaded0"), sem("res_loaded1")]
        out_ready = sem("out_ready")
        out_free = [sem("out_free0"), sem("out_free1")]

        W_PARTS = [slice(n * C + lo, n * C + hi) for lo, hi in ((0, P), (P, C)) for n in range(3)]

        def x_of(b, n):
            if is_batch(b, -1):
                return x_first[:, n % CT, n // CT * HALF:(n // CT + 1) * HALF]
            return x_in[:, n % X_BUFS, :]

        def first_bank(i):
            return scores[:, 1, 0:HALF] if i >= 2 and i % 2 == 0 else dense[:, :]

        def last_proj_bank(part):
            return scores[:, 0, 0:HALF] if part % 2 == 0 else dense[:, :]

        def proj_place(b, part):
            if is_batch(b, B):
                return part % CT, part // CT * HALF
            return part // 2, part % 2 * HALF

        block = ctx.enter_context(nc.Block())

        def in_loop(engine, batch):
            batch(0, True, False)
            with engine.Fori(1, B - 1) as b:
                batch(b, False, False)
            batch(B - 1, False, True)

        @block.tensor
        def _(pe):
            def split_product(dst, w, r, n, count):
                for j, (i, k) in enumerate(((0, 0), (1, 0), (0, 1))):
                    last = nc.tensor.matmul(dst, w(i), r(k), start=n == 0 and j == 0, stop=n == count - 1 and j == 2)
                return last

            def wait_bank_left(b, before):
                _, kind, pair, part = before
                if kind == "p":
                    pe.wait_ge(proj_biased, N_PROJ * b - N_PROJ + part + 1)
                elif kind == "g":
                    pe.wait_ge(gn_done, 20 * b + (33, 37)[part])
                else:
                    pe.wait_ge(qkv_full, 24 * b + 6 * pair + QKV.index((kind, part)) + 1)

            def dense_chunk(b, chunk, bank):
                _, kind, pair, part = chunk
                h = pair % CT
                if kind == "g":
                    pe.wait_ge(gn_done, 20 * b + (32, 36)[part])
                    src = mean_var[:, :, 0] if part == 0 else c_var[:, :]
                    last = nc.tensor.matmul(bank[:, 0:CT], group_mean[:, :], src, start=True, stop=True)
                elif kind == "v":
                    if is_batch(b, -1) and part == 0:
                        pe.wait_ge(w_ready, 3)
                    for s in range(4):
                        k0 = (4 * part + s) * P
                        for c in range(CT):
                            last = split_product(bank[:, s * P:(s + 1) * P], lambda i: xn[:, i, c, k0:k0 + P],
                                                 lambda i: w_qkv[:, i, c, 2 * C + h * P:2 * C + (h + 1) * P], c, CT)
                elif kind == "p":
                    o, n0 = proj_place(b, part)
                    if part == 0:
                        pe.wait_ge(att_lo, HB * B - 1 if is_batch(b, B) else HB * b)
                        pe.wait_ge(att_moved, 16 * b)
                        pe.wait_ge(w_ready, len(W_PARTS) + 1)
                    if is_batch(b, B) and part == CT:
                        pe.wait_ge(att_lo, HB * B)
                    for c in range(CT):
                        last = split_product(bank, lambda i: w_proj[:, i, c, o * P:(o + 1) * P],
                                             lambda i: att[:, i, c, n0:n0 + HALF], c, CT)
                else:
                    if kind == "q" and pair == 4:
                        pe.wait_ge(xn_lo, 8 * b + 8 + 4 * (part + 1))
                    if is_batch(b, -1) and part == 0:
                        pe.wait_ge(w_ready, 1 if kind == "q" else 2)
                    o = (0 if kind == "q" else C) + h * P
                    for c in range(CT):
                        last = split_product(bank, lambda i: w_qkv[:, i, c, o:o + P],
                                             lambda i: xn[:, i, c, part * HALF:(part + 1) * HALF], c, CT)
                last.then_inc(dense_done, 1)

            def score_tile(t):
                buf, head, q0 = t // NT % 2, t % 2, t % NT // 2 * P
                for bank in range(2):
                    for part in range(2):
                        last = nc.tensor.matmul(scores[:, t % 2, bank * HALF:(bank + 1) * HALF],
                                                q_st[:, buf, head, q0:q0 + P],
                                                k_st[:, buf, head, part, bank * HALF:(bank + 1) * HALF],
                                                start=part == 0, stop=part == 1)
                last.then_inc(scores_ready, 1)

            def attend(t, s):
                half = t // 8 - 1
                buf = half // 2 % 2
                for j, (i, k) in enumerate(((0, 0), (1, 0), (0, 1))):
                    for head in range(2):
                        last = nc.tensor.matmul(att_acc[head * HD:(head + 1) * HD, :],
                                                v_sb[:, buf, s, i, head * HD:(head + 1) * HD],
                                                pT[:, half % 2, k, s, head, :],
                                                start=s == 0 and j == 0, stop=s == ST - 1 and j == 2)
                if s == ST - 1:
                    last.then_inc(att_done, 1)

            def turn_rows():
                nc.tensor.transpose(dense[0:8, 0:P], recip[:, :], ident[:, :]).then_inc(rows_turned, 1)

            def batch(b, first, final):
                for t in range(TB):
                    pe.wait_ge(probs_ready, TB * b + t + 1)
                    if not (final and t + 2 >= TB):
                        if (t + 2) % NT == 0:
                            pair = (t + 2) // NT
                            pe.wait_ge(q_stacked, 64 * CT * b + 64 * (pair + 1))
                            pe.wait_ge(k_stacked, 64 * CT * b + 64 * (pair + 1))
                        score_tile(t + 2)
                    for bank in range(2):
                        if begun(count := 2 * TB * b + 2 * t + bank - 1):
                            pe.wait_ge(pT_lo, count)
                        for s in range(4):
                            k0 = (4 * bank + s) * P
                            last = nc.tensor.transpose(turned[:, bank, s * P:(s + 1) * P],
                                                       probs[:, t % 2, k0:k0 + P], ident[:, :])
                        last.then_inc(turned_ready, 1)
                    for i, chunk in dense_of(first, final):
                        if chunk[0] == t:
                            if i == 0:
                                wait_bank_left(b - 1, BEFORE[-1])
                                if first:
                                    pe.wait_ge(w_ready, len(W_PARTS))
                            else:
                                wait_bank_left(b, dense_of(first, final)[i - 1][1])
                            rows = (t - 4) // 8
                            if not (first and rows < 1) and (i == 0 or dense_of(first, final)[i - 1][1][0] <= 8 * rows + 3):
                                pe.wait_ge(rows_kept, HB * b + rows)
                            dense_chunk(b, chunk, dense[:, :])
                    if not (first and t < 8):
                        dense_steps = [chunk[0] for _, chunk in dense_of(first, final)]
                        s = t % 8
                        if t // 2 * 2 in dense_steps:
                            blocks = [s - 1, s] if t % 2 else []
                        else:
                            blocks = [s]
                        if 0 in blocks:
                            pe.wait_ge(pT_lo, 2 * TB * b + 2 * (t - s))
                            if begun(count := HB * b + t // 8 - 1):
                                pe.wait_ge(att_scaled, count)
                            if t % NT >= 8:
                                pe.wait_ge(qkv_lo, 24 * b + 6 * (t // NT) + 6)
                        for block_of_keys in blocks:
                            attend(t, block_of_keys)
                        if t % 8 == 3:
                            pe.wait_ge(recip_ready, HB * b + t // 8)
                            wait_bank_left(b, [chunk for _, chunk in dense_of(first, final) if chunk[0] <= t][-1])
                            turn_rows()

            pe.wait_ge(const_ready, 1)
            for i, chunk in enumerate(BEFORE):
                if i:
                    wait_bank_left(-1, BEFORE[max(i - 2, 0)])
                dense_chunk(-1, chunk, first_bank(i))
            wait_bank_left(-1, BEFORE[-2])
            pe.wait_ge(q_stacked, 64)
            pe.wait_ge(k_stacked, 64)
            score_tile(0)
            score_tile(1)
            in_loop(pe, batch)
            pe.wait_ge(recip_ready, HB * B)
            wait_bank_left(B - 1, dense_of(False, True)[-1][1])
            turn_rows()
            pe.wait_ge(pT_lo, 2 * TB * B)
            pe.wait_ge(att_scaled, HB * B - 1)
            for s in range(ST):
                attend(TB, s)
            for part in range(N_PROJ):
                if part == 1:
                    pe.wait_ge(rows_kept, HB * B)
                elif part >= 2:
                    pe.wait_ge(proj_biased, N_PROJ * (B - 1) + part - 1)
                dense_chunk(B, (0, "p", 0, part), last_proj_bank(part))

        @block.scalar
        def _(act):
            def drain_dense(b, number, chunk, bank=dense):
                _, kind, pair, part = chunk
                if kind == "g":
                    return
                h = pair % CT
                act.wait_ge(dense_done, number + 1)
                if kind == "p":
                    o, _ = proj_place(b, part)
                    act.wait_ge(out_free[part % 2], 64 * b - 48 + 16 * (part // 2))
                    nc.scalar.activation(out_sb[:, part % 2, :], bank[:, :], ACT.Identity,
                                         bias=projb_sb[:, o:o + 1], scale=QKV_SCALE)\
                        .then_inc(proj_biased, 1)
                    return
                n = QKV.index((kind, part))
                if begun(count := 24 * b + 6 * pair + n - 1):
                    act.wait_ge(qkv_lo, count)
                if kind == "q":
                    scale, bias = QKV_SCALE * ATT_SCALE, qb_scaled[:, h:h + 1]
                elif kind == "k":
                    scale, bias = QKV_SCALE, qkvb_sb[:, CT + h:CT + h + 1]
                else:
                    scale, bias = QKV_SCALE, 0.0
                nc.scalar.activation(qkv32[:, n % 2, :], bank[:, :], ACT.Identity, bias=bias, scale=scale)\
                    .then_inc(qkv_full, 1)

            def normal_hi(b, n):
                c, part = n % CT, n // CT
                act.wait_ge(x_normal, 8 * b + 8 + n + 1)
                nc.scalar.activation(xn[:, 0, c, part * HALF:(part + 1) * HALF], x_of(b, n), ACT.Copy)\
                    .then_inc(xn_hi, 1)

            def exp_tile(b, t):
                act.wait_ge(max_ready, TB * b + t + 1)
                if t % 8 == 0:
                    if begun(count := HB * b + t // 8 - 1):
                        act.wait_ge(recip_ready, count)
                nc.scalar.activation(probs[:, t % 2, :], scores[:, t % 2, :], ACT.Exp,
                                     bias=neg_max[:, t % 4:t % 4 + 1],
                                     accum_out=row_sum[:, t // 8 % 2, t % 8:t % 8 + 1]).then_inc(probs_ready, 1)

            def turned_hi(b, t, bank):
                act.wait_ge(turned_ready, 2 * TB * b + 2 * t + bank + 1)
                if t % 8 == 0 and bank == 0:
                    if begun(count := HB * b + t // 8 - 1):
                        act.wait_ge(att_done, count)
                q0 = t % 8 // 2 * P
                nc.scalar.activation(pT[:, t // 8 % 2, 0, 4 * bank:4 * bank + 4, t % 2, q0:q0 + P],
                                     turned[:, bank, :].rearrange("p (s q) -> p s q", q=P), ACT.Copy).then_inc(pT_hi, 1)

            def keep_rows(b, half):
                act.wait_ge(rows_turned, HB * b + half + 1)
                nc.scalar.activation(recip_turned[:, :], dense[0:8, 0:P], ACT.Copy).then_inc(rows_kept, 1)

            def batch(b, first, final):
                for t in range(TB):
                    if t % 8 == 4 and not (first and t < 8):
                        keep_rows(b, t // 8 - 1)
                    for bank in range(2):
                        turned_hi(b, t, bank)
                    if not (final and t + 2 >= TB):
                        exp_tile(b, t + 2)
                    for i, chunk in dense_of(first, final):
                        if chunk[0] == t:
                            drain_dense(b, dense_base(b) + i, chunk)
                    if not final and t - 1 in NORMALISE_STEPS:
                        n = NORMALISE_STEPS.index(t - 1)
                        if n % CT == 0:
                            act.wait_ge(dense_done, dense_base(b) + place_of(first, final, "v", 3, n // CT) + 1)
                        normal_hi(b, n)
                    if first and t == 8:
                        act.wait_ge(w_proj_loaded, 16)
                        nc.scalar.activation(w_proj[:, 0, :, :], w_proj_in, ACT.Copy, scale=W_SCALE).then_inc(w_hi, 1)

            def weights_hi(n):
                act.wait_ge(w_loaded[n], 16)
                nc.scalar.activation(w_qkv[:, 0, :, W_PARTS[n]], w_qkv_in[:, :, W_PARTS[n]], ACT.Copy, scale=W_SCALE)\
                    .then_inc(w_hi, 1)

            act.wait_ge(small_in, 48)
            act.wait_ge(out_free[0], 16)
            act.wait_ge(out_free[1], 16)
            nc.scalar.mul(qb_scaled[:, :], qkvb_sb[:, 0:CT], ATT_SCALE).then_inc(bias_ready, 1)
            for n in range(2 * CT):
                normal_hi(-1, n)
                if n in (1, 3, 5):
                    weights_hi(n // 2)
            act.wait_ge(bias_ready, 1)
            for i, chunk in enumerate(BEFORE):
                drain_dense(-1, i, chunk, first_bank(i))
                if 2 <= i < 5:
                    weights_hi(i + 1)
            exp_tile(0, 0)
            exp_tile(0, 1)
            in_loop(act, batch)
            keep_rows(B - 1, HB - 1)
            base = PER_BATCH * (B - 1) + len(dense_of(False, True))
            for part in range(N_PROJ):
                drain_dense(B, base + part, (0, "p", 0, part), last_proj_bank(part))

        @block.vector
        def _(dve):
            def gn_stats(b, n):
                buf = n % X_BUFS
                dve.wait_ge(x_loaded[buf], 64 * b + 32 + 16 * (n // X_BUFS))
                nc.vector.bn_stats(stats[:, n // 2, n % 2, :], x_in[:, buf, :]).then_inc(gn_done, 1)

            def gn_stats_first(c):
                dve.wait_ge(x_loaded[c], 16)
                for n in range(2):
                    nc.vector.bn_stats(stats[:, c, n, :], x_first[:, c, n * HALF:(n + 1) * HALF]).then_inc(gn_done, 1)

            def gn_aggregate(c):
                nc.vector.bn_aggr(mean_var[:, c, :], stats[:, c, :, :]).then_inc(gn_done, 1)

            def gn_mean(b, number):
                n0 = 20 * b + 20
                dve.wait_ge(dense_done, number + 1)
                nc.vector.tensor_copy(g_mean[:, :], dense[:, 0:CT]).then_inc(gn_done, 1)
                dve.wait_ge(gn_done, n0 + 13)
                nc.vector.tensor_tensor(dev[:, :], mean_var[:, :, 0], g_mean[:, :], ALU.subtract).then_inc(gn_done, 1)
                dve.wait_ge(gn_done, n0 + 14)
                nc.vector.tensor_tensor(dev2[:, :], dev[:, :], dev[:, :], ALU.mult).then_inc(gn_done, 1)
                dve.wait_ge(gn_done, n0 + 15)
                nc.vector.tensor_tensor(c_var[:, :], dev2[:, :], mean_var[:, :, 1], ALU.add).then_inc(gn_done, 1)

            def gn_affine(b, number):
                n0 = 20 * b + 20
                dve.wait_ge(dense_done, number + 1)
                nc.vector.tensor_scalar(g_var[:, :], dense[:, 0:CT], EPS, None, ALU.add)\
                    .then_inc(gn_done, 1)
                dve.wait_ge(rstd_ready, b + 2)
                nc.vector.tensor_tensor(xn_scale[:, :], rstd[:, :], g_sb[:, :], ALU.mult).then_inc(gn_done, 1)
                dve.wait_ge(gn_done, n0 + 18)
                nc.vector.tensor_tensor(mean_scaled[:, :], g_mean[:, :], xn_scale[:, :], ALU.mult).then_inc(gn_done, 1)
                dve.wait_ge(gn_done, n0 + 19)
                nc.vector.tensor_tensor(xn_shift[:, :], b_sb[:, :], mean_scaled[:, :], ALU.subtract).then_inc(gn_done, 1)

            def max_tile(b, t):
                dve.wait_ge(scores_ready, TB * b + t + 1)
                nc.vector.tensor_reduce(neg_max[:, t % 4:t % 4 + 1], scores[:, t % 2, :], AX.X, ALU.max,
                                        negate=True).then_inc(max_ready, 1)

            def turned_lo(b, t, bank):
                dve.wait_ge(pT_hi, 2 * TB * b + 2 * t + bank + 1)
                q0 = t % 8 // 2 * P
                part = [pT[:, t // 8 % 2, i, 4 * bank:4 * bank + 4, t % 2, q0:q0 + P] for i in range(2)]
                nc.vector.tensor_tensor(part[1], turned[:, bank, :].rearrange("p (s q) -> p s q", q=P), part[0],
                                        ALU.subtract).then_inc(pT_lo, 1)

            def scale_att(b, half):
                dve.wait_ge(att_done, HB * b + half + 1)
                dve.wait_ge(rows_in, 32 * (HB * b + half + 1))
                if begun(count := HB * b + half):
                    dve.wait_ge(att_lo, count)
                nc.vector.tensor_tensor(att32[:, :], att_acc[:, :], recip_rows[:, :], ALU.mult).then_inc(att_scaled, 1)

            def bias_att(b, half):
                pair = half // 2
                dve.wait_ge(att_scaled, HB * b + half + 1)
                nc.vector.tensor_scalar(att32[:, :], att32[:, :], qkvb_sb[:, 2 * CT + pair:2 * CT + pair + 1], None,
                                        ALU.add).then_inc(att_biased, 1)

            def att_split_hi(b, half, att_read=0):
                pair, n0 = half // 2, half % 2 * HALF
                dve.wait_ge(att_biased, HB * b + half + 1)
                if half == 0 and begun(count := 16 * b):
                    dve.wait_ge(att_moved, count)
                if begun(att_read):
                    dve.wait_ge(dense_done, att_read)
                dst = att_first[:, 0, n0:n0 + HALF] if pair == 0 else att[:, 0, pair, n0:n0 + HALF]
                nc.vector.tensor_copy(dst, att32[:, :]).then_inc(att_hi, 1)

            def qkv_split_hi(b, chunk):
                _, kind, pair, part = chunk
                n = QKV.index((kind, part))
                dve.wait_ge(qkv_full, 24 * b + 6 * pair + n + 1)
                if kind == "v":
                    if begun(count := HB * b + 2 * pair - 2):
                        dve.wait_ge(att_done, count)
                    full = qkv32[:, n % 2, :].rearrange("p (s c) -> p s c", c=P)
                    hi = v_sb[:, pair % 2, 4 * part:4 * part + 4, 0, :]
                else:
                    nat, stacked = (q_nat, q_stacked) if kind == "q" else (k_nat, k_stacked)
                    if begun(count := 64 * CT * b + 64 * pair):
                        dve.wait_ge(stacked, count)
                    full, hi = qkv32[:, n % 2, :], nat[:, 0, part * HALF:(part + 1) * HALF]
                nc.vector.tensor_copy(hi, full).then_inc(qkv_hi, 1)

            def normalise(b, n):
                c, part, buf = n % CT, n // CT, n % X_BUFS
                if not (is_batch(b, -1)):
                    dve.wait_ge(x_loaded[buf], 64 * b + 64 + 16 * part)
                dve.wait_ge(gn_done, 20 * b + 40)
                nc.vector.tensor_scalar(x_of(b, n), x_of(b, n), xn_scale[:, c:c + 1], xn_shift[:, c:c + 1],
                                        ALU.mult, ALU.add).then_inc(x_normal, 1)

            def invert_sums(b, half):
                dve.wait_ge(probs_ready, TB * b + 8 * half + 8)
                if begun(count := HB * b + half):
                    dve.wait_ge(rows_turned, count)
                nc.vector.reciprocal(recip[:, :], row_sum[:, half % 2, :]).then_inc(recip_ready, 1)

            def batch(b, first, final):
                for t in range(TB):
                    if t % 8 == 0 and not (first and t < 16):
                        if t >= 16:
                            scale_att(b, t // 8 - 2)
                        else:
                            scale_att(b - 1, HB - 2 + t // 8)
                    aggregate = not final and t - 1 in STATS_STEPS[1::2]
                    if aggregate:
                        c = STATS_STEPS.index(t - 1) // 2
                        dve.wait_ge(gn_done, 20 * b + 20 + 3 * c + 2)
                    if not (final and t + 2 >= TB):
                        max_tile(b, t + 2)
                    if aggregate:
                        gn_aggregate(c)
                    for bank in range(2):
                        turned_lo(b, t, bank)
                    if t % 8 in (0, 1) and not (first and t < 16):
                        at_batch, half = (b, t // 8 - 2) if t >= 16 else (b - 1, HB - 2 + t // 8)
                        if t % 8 == 0:
                            bias_att(at_batch, half)
                        elif t == 33 and not first:
                            att_split_hi(b, 2, dense_base(b) + place_of(first, final, "p", 0, 7) + 1)
                        else:
                            att_split_hi(at_batch, half)
                    for i, chunk in dense_of(first, final):
                        if chunk[0] + 1 == t and chunk[1] in "qkv":
                            qkv_split_hi(b, chunk)
                    if not final and t in NORMALISE_STEPS:
                        normalise(b, NORMALISE_STEPS.index(t))
                    if t % 8 == 0 and not (first and t < 8):
                        if t >= 8:
                            invert_sums(b, t // 8 - 1)
                        else:
                            invert_sums(b - 1, HB - 1)
                    if not final and t in STATS_STEPS:
                        gn_stats(b, STATS_STEPS.index(t))
                    for i, chunk in dense_of(first, final):
                        if chunk[0] == t and chunk[1] == "g":
                            (gn_mean, gn_affine)[chunk[3]](b, dense_base(b) + i)
                    if first and t == 9:
                        dve.wait_ge(w_hi, len(W_PARTS) + 1)
                        nc.vector.scalar_tensor_tensor(w_proj[:, 1, :, :], w_proj_in, W_SCALE, w_proj[:, 0, :, :],
                                                       ALU.mult, ALU.subtract).then_inc(w_ready, 1)

            def weights_lo(n):
                dve.wait_ge(w_hi, n + 1)
                nc.vector.scalar_tensor_tensor(w_qkv[:, 1, :, W_PARTS[n]], w_qkv_in[:, :, W_PARTS[n]], W_SCALE,
                                               w_qkv[:, 0, :, W_PARTS[n]], ALU.mult, ALU.subtract).then_inc(w_ready, 1)

            for c in range(CT):
                gn_stats_first(c)
                dve.wait_ge(gn_done, 3 * c + 2)
                gn_aggregate(c)
            dve.wait_ge(small_in, 48)
            gn_mean(-1, 0)
            gn_affine(-1, 1)
            for n in range(2 * CT):
                normalise(-1, n)
                if n in (3, 5, 7):
                    weights_lo(n // 2 - 1)
            for i, chunk in enumerate(BEFORE[2:]):
                qkv_split_hi(-1, chunk)
                if i < 3:
                    weights_lo(i + 3)
            max_tile(0, 0)
            max_tile(0, 1)
            in_loop(dve, batch)
            scale_att(B - 1, HB - 2)
            invert_sums(B - 1, HB - 1)
            bias_att(B - 1, HB - 2)
            att_split_hi(B - 1, HB - 2)
            scale_att(B - 1, HB - 1)
            bias_att(B - 1, HB - 1)
            att_split_hi(B - 1, HB - 1)

        @block.gpsimd
        def _(pool):
            def qkv_split_lo(b, chunk):
                _, kind, pair, part = chunk
                n = QKV.index((kind, part))
                pool.wait_ge(qkv_hi, 24 * b + 6 * pair + n + 1)
                if kind == "v":
                    full = qkv32[:, n % 2, :].rearrange("p (s c) -> p s c", c=P)
                    hi, lo = (v_sb[:, pair % 2, 4 * part:4 * part + 4, i, :] for i in range(2))
                else:
                    nat = q_nat if kind == "q" else k_nat
                    full = qkv32[:, n % 2, :]
                    hi, lo = (nat[:, i, part * HALF:(part + 1) * HALF] for i in range(2))
                nc.gpsimd.tensor_tensor(lo, full, hi, ALU.subtract).then_inc(qkv_lo, 1)

            def xn_split_lo(b, n):
                c, at = n % CT, slice(n // CT * HALF, (n // CT + 1) * HALF)
                pool.wait_ge(xn_hi, 8 * b + 8 + n + 1)
                nc.gpsimd.tensor_tensor(xn[:, 1, c, at], x_of(b, n), xn[:, 0, c, at], ALU.subtract)\
                    .then_inc(xn_lo, 1)

            def att_split_lo(b, half):
                pair, n0 = half // 2, half % 2 * HALF
                pool.wait_ge(att_hi, HB * b + half + 1)
                hi, lo = ((att_first[:, i, n0:n0 + HALF] if pair == 0 else att[:, i, pair, n0:n0 + HALF]) for i in range(2))
                nc.gpsimd.tensor_tensor(lo, att32[:, :], hi, ALU.subtract).then_inc(att_lo, 1)

            def add_residual(b, part):
                pool.wait_ge(res_loaded[part % 2], 64 * b - 64 + 16 * (part // 2) + 16)
                pool.wait_ge(proj_biased, N_PROJ * b - N_PROJ + part + 1)
                nc.gpsimd.tensor_tensor(out_sb[:, part % 2, :], out_sb[:, part % 2, :], resid[:, part % 2, :], ALU.add)\
                    .then_inc(out_ready, 1)

            def invert_std(b):
                pool.wait_ge(gn_done, 20 * b + 37)
                nc.gpsimd.tensor_tensor(rstd[:, :], g_var[:, :], minus_half[:, :], ALU.pow).then_inc(rstd_ready, 1)

            def batch(b, first, final):
                for t in range(TB):
                    for i, chunk in dense_of(first, final):
                        if chunk[0] + 1 == t and chunk[1] in "qkv":
                            qkv_split_lo(b, chunk)
                        if chunk[0] == t:
                            if chunk[1] == "p":
                                add_residual(b, chunk[3])
                            elif chunk[1] == "g" and chunk[3] == 1:
                                invert_std(b)
                    if t % 8 == 1 and not (first and t < 16):
                        if t >= 16:
                            att_split_lo(b, t // 8 - 2)
                        else:
                            att_split_lo(b - 1, HB - 2 + t // 8)
                    if not final and t - 1 in NORMALISE_STEPS:
                        xn_split_lo(b, NORMALISE_STEPS.index(t - 1))

            nc.gpsimd.memset(ident[:, :], 0.0).then_inc(const_steps, 1)
            nc.gpsimd.memset(group_mean[:, :], GROUPS / C).then_inc(const_steps, 1)
            nc.gpsimd.memset(minus_half[:, :], -0.5).then_inc(const_steps, 1)
            pool.wait_ge(const_steps, 3)
            nc.gpsimd.affine_select(out=ident[:, :], in_=ident[:, :], compare_op=ALU.not_equal, fill=1.0, base=0,
                                    pattern=[[-1, P]], channel_multiplier=1).then_inc(const_steps, 1)
            per = C // GROUPS
            blocks = group_mean[:, :].rearrange("p (g c) -> p g c", c=per)
            nc.gpsimd.affine_select(out=blocks, in_=blocks, compare_op=ALU.is_ge, fill=0.0, base=0,
                                    pattern=[[-per, P // per], [0, per]], channel_multiplier=1).then_inc(const_steps, 1)
            pool.wait_ge(const_steps, 5)
            nc.gpsimd.affine_select(out=blocks, in_=blocks, compare_op=ALU.is_ge, fill=0.0, base=per - 1,
                                    pattern=[[per, P // per], [0, per]], channel_multiplier=-1).then_inc(const_ready, 1)
            invert_std(-1)
            for n in range(2 * CT):
                xn_split_lo(-1, n)
            for chunk in BEFORE[2:]:
                qkv_split_lo(-1, chunk)
            in_loop(pool, batch)
            att_split_lo(B - 1, HB - 2)
            att_split_lo(B - 1, HB - 1)
            for part in range(N_PROJ):
                add_residual(B, part)

        @block.sync
        def _(sp):
            def row(ap, b):
                return ap[bass.ds(b, 1)].rearrange("o c s -> (o c) s")

            def load_x(b, k):
                buf = k % X_BUFS
                c, part = (k // 2, k % 2) if k < 8 else (k % CT, (k - 8) // CT)
                if k < 4:
                    if not is_batch(b, 0):
                        sp.wait_ge(xn_lo, 8 * b + 5 + k)
                elif k < 12:
                    sp.wait_ge(gn_done, 20 * b + 20 + 3 * ((k - 4) // 2) + 1 + (k - 4) % 2)
                else:
                    sp.wait_ge(xn_lo, 8 * b + 8 + k - 11)
                sp.dma_start(x_in[:, buf, :], row(x, b + 1)[c * P:(c + 1) * P, part * HALF:(part + 1) * HALF])\
                    .then_inc(x_loaded[buf], 16)

            def stack_q(b, pair):
                buf, h = pair % 2, HD
                sp.wait_ge(qkv_lo, 24 * b + 6 * pair + 3)
                for dst, head, src, part in ((0, 0, 0, 0), (h, 0, 0, 1), (0, 1, h, 1), (h, 1, h, 0)):
                    sp.dma_start(q_st[dst:dst + h, buf, head, :], q_nat[src:src + h, part, :]).then_inc(q_stacked, 16)

            def stack_k(b, pair):
                buf, h = pair % 2, HD
                sp.wait_ge(qkv_lo, 24 * b + 6 * pair + 4)
                for head in range(2):
                    for dst in (0, h):
                        sp.dma_start(k_st[dst:dst + h, buf, head, :, :], k_nat[head * h:(head + 1) * h, :, :])\
                            .then_inc(k_stacked, 16)

            def load_residual(b, part):
                o, n0 = proj_place(b, part)
                if part < 2:
                    sp.wait_ge(out_free[part], 64 * b - 48)
                else:
                    sp.wait_ge(out_ready, N_PROJ * b - N_PROJ + part - 1)
                sp.dma_start(resid[:, part % 2, :], row(x, b - 1)[o * P:(o + 1) * P, n0:n0 + HALF])\
                    .then_inc(res_loaded[part % 2], 16)

            def store(b, part):
                o, n0 = proj_place(b, part)
                sp.wait_ge(out_ready, N_PROJ * b - N_PROJ + part + 1)
                sp.dma_start(row(out, b - 1)[o * P:(o + 1) * P, n0:n0 + HALF], out_sb[:, part % 2, :])\
                    .then_inc(out_free[part % 2], 16)

            def move_first(b, first, final):
                sp.wait_ge(att_lo, HB * b + 2)
                if not first:
                    sp.wait_ge(dense_done, dense_base(b) + place_of(first, final, "p", 0, 7) + 1)
                sp.dma_start(att[:, :, 0, :], att_first[:, :, :]).then_inc(att_moved, 16)

            def spread_rows(b, half):
                sp.wait_ge(rows_kept, HB * b + half + 1)
                sp.dma_start(recip_dram, recip_turned[:, :]).then_inc(rows_out, 16)
                sp.wait_ge(rows_out, 16 * (HB * b + half + 1))
                by_head = recip_dram.rearrange("(q h) c -> h q c", h=2)
                for head in range(2):
                    sp.dma_start(recip_rows[head * HD:(head + 1) * HD, :].rearrange("p (q c) -> p q c", c=P),
                                 by_head[head].partition_broadcast(HD)).then_inc(rows_in, 16)

            def batch(b, first, final):
                for t in range(TB):
                    if t % 8 == 4 and not (first and t < 8):
                        spread_rows(b, t // 8 - 1)
                    for i, chunk in dense_of(first, final):
                        at, kind, pair, part = chunk
                        if at + 2 == t and kind in "qk" and part == 1:
                            (stack_q if kind == "q" else stack_k)(b, pair)
                        if at + 1 == t and kind == "p":
                            store(b, part)
                        if at - 1 == t and kind == "p":
                            load_residual(b, part)
                    if not final and t in X_STEPS:
                        for k in [k for k, s in enumerate(X_STEPS) if s == t]:
                            load_x(b, k)
                    if t == 33:
                        move_first(b, first, final)

            for c in range(CT):
                sp.dma_start(x_first[:, c, :], row(x, 0)[c * P:(c + 1) * P, :]).then_inc(x_loaded[c], 16)
            for dst, src in ((g_sb, norm_g), (b_sb, norm_b), (qkvb_sb, qkv_b)):
                sp.dma_start(dst[:, :], src).then_inc(small_in, 16)
            for n in range(2):
                cols = slice(n * CT // 2, (n + 1) * CT // 2)
                sp.dma_start(projb_sb[:, cols], proj_b[:, cols]).then_inc(out_free[n], 16)
            by_tile = qkv_wT.rearrange("(c p) o -> p c o", p=P)
            for n in range(len(W_PARTS)):
                sp.dma_start(w_qkv_in[:, :, W_PARTS[n]], by_tile[:, :, W_PARTS[n]]).then_inc(w_loaded[n], 16)
            stack_q(-1, 4)
            stack_k(-1, 4)
            sp.dma_start(w_proj_in, proj_wT.rearrange("(c p) o -> p c o", p=P)).then_inc(w_proj_loaded, 16)
            in_loop(sp, batch)
            spread_rows(B - 1, HB - 1)
            for part in range(2):
                load_residual(B, part)
            for part in range(N_PROJ):
                store(B, part)
                if part + 2 < N_PROJ:
                    load_residual(B, part + 2)
            for buf in range(2):
                sp.wait_ge(out_free[buf], 16 + 64 * B)


def kernel(**inputs):
    import numpy as np
    import concourse.bacc as bacc
    from concourse.bass_utils import run_bass_kernel_spmd

    x = np.asarray(inputs["x"])
    B, C, H, W = x.shape

    def columns(v):
        return np.ascontiguousarray(np.asarray(v).reshape(-1, P).T)

    arrays = {
        "x": np.ascontiguousarray(x.reshape(B, C, H * W)),
        "norm_g": columns(inputs["L0_conv_norm_g"]),
        "norm_b": columns(inputs["L0_conv_norm_b"]),
        "qkv_wT": np.ascontiguousarray(np.asarray(inputs["L0_conv_qkv_w"]).T),
        "qkv_b": columns(inputs["L0_conv_qkv_b"]),
        "proj_wT": np.ascontiguousarray(np.asarray(inputs["L0_conv_proj_w"]).T),
        "proj_b": columns(inputs["L0_conv_proj_b"]),
    }
    nc = bacc.Bacc("TRN2", target_bir_lowering=False, num_devices=1)
    args = [nc.dram_tensor(n, a.shape, F32, kind="ExternalInput").ap() for n, a in arrays.items()]
    out = nc.dram_tensor("out", (B, C, H * W), F32, kind="ExternalOutput").ap()
    attention_block(nc, *args, out)
    result = run_bass_kernel_spmd(nc, [arrays], core_ids=[0])
    return result.results[0]["out"].reshape(B, C, H, W)
```
